# Optimizing a Trainium2 kernel written in Bass

```python
import numpy as np
import jax
import jax.numpy as jnp

def _softmax(x, axis=-1):
    return jax.nn.softmax(x, axis=axis)

def _gelu(x):
    return jax.nn.gelu(x, approximate=True)

def _silu(x):
    return jax.nn.silu(x)

def _sigmoid(x):
    return jax.nn.sigmoid(x)

def _layernorm(x, axis=-1, eps=1e-05):
    m = jnp.mean(x, axis=axis, keepdims=True)
    v = jnp.var(x, axis=axis, keepdims=True)
    return (x - m) / jnp.sqrt(v + eps)

def _scatter_add(tgt, idx, src, axis=0):
    return tgt.at[idx].add(src)

def _segment_sum(src, seg, n):
    return jax.ops.segment_sum(src, seg, n)
kernel_name = 'mk_rec_standalone_d1_rec_r8_c0e6f3'

def setup_inputs(seed: int=0):
    np.random.seed(seed)
    _w = jnp.asarray

    def _rec_inputs():
        import jax
        import jax.numpy as jnp
        _rk = jax.random.key(seed)
        r_num = -0.000520686 + 1.00062 * jax.random.normal(jax.random.fold_in(_rk, 1), (512, 256), jnp.float32)
        r_cat = jnp.stack([jax.random.randint(jax.random.fold_in(jax.random.fold_in(_rk, 2), 0), (512,), 19, 199963, jnp.int32), jax.random.randint(jax.random.fold_in(jax.random.fold_in(_rk, 2), 1), (512,), 7, 199982, jnp.int32), jax.random.randint(jax.random.fold_in(jax.random.fold_in(_rk, 2), 2), (512,), 0, 199989, jnp.int32), jax.random.randint(jax.random.fold_in(jax.random.fold_in(_rk, 2), 3), (512,), 43, 199994, jnp.int32), jax.random.randint(jax.random.fold_in(jax.random.fold_in(_rk, 2), 4), (512,), 20, 24999, jnp.int32), jax.random.randint(jax.random.fold_in(jax.random.fold_in(_rk, 2), 5), (512,), 12, 199986, jnp.int32), jax.random.randint(jax.random.fold_in(jax.random.fold_in(_rk, 2), 6), (512,), 2, 199999, jnp.int32), jax.random.randint(jax.random.fold_in(jax.random.fold_in(_rk, 2), 7), (512,), 35, 199995, jnp.int32), jax.random.randint(jax.random.fold_in(jax.random.fold_in(_rk, 2), 8), (512,), 4, 199954, jnp.int32), jax.random.randint(jax.random.fold_in(jax.random.fold_in(_rk, 2), 9), (512,), 3, 199986, jnp.int32), jax.random.randint(jax.random.fold_in(jax.random.fold_in(_rk, 2), 10), (512,), 15, 24997, jnp.int32), jax.random.randint(jax.random.fold_in(jax.random.fold_in(_rk, 2), 11), (512,), 15, 199973, jnp.int32), jax.random.randint(jax.random.fold_in(jax.random.fold_in(_rk, 2), 12), (512,), 12, 199989, jnp.int32), jax.random.randint(jax.random.fold_in(jax.random.fold_in(_rk, 2), 13), (512,), 59, 199989, jnp.int32), jax.random.randint(jax.random.fold_in(jax.random.fold_in(_rk, 2), 14), (512,), 2, 199959, jnp.int32), jax.random.randint(jax.random.fold_in(jax.random.fold_in(_rk, 2), 15), (512,), 23, 199981, jnp.int32), jax.random.randint(jax.random.fold_in(jax.random.fold_in(_rk, 2), 16), (512,), 0, 199998, jnp.int32), jax.random.randint(jax.random.fold_in(jax.random.fold_in(_rk, 2), 17), (512,), 13, 199983, jnp.int32), jax.random.randint(jax.random.fold_in(jax.random.fold_in(_rk, 2), 18), (512,), 48, 199980, jnp.int32), jax.random.randint(jax.random.fold_in(jax.random.fold_in(_rk, 2), 19), (512,), 18, 199993, jnp.int32), jax.random.randint(jax.random.fold_in(jax.random.fold_in(_rk, 2), 20), (512,), 0, 199995, jnp.int32), jax.random.randint(jax.random.fold_in(jax.random.fold_in(_rk, 2), 21), (512,), 1, 199990, jnp.int32), jax.random.randint(jax.random.fold_in(jax.random.fold_in(_rk, 2), 22), (512,), 25, 24998, jnp.int32), jax.random.randint(jax.random.fold_in(jax.random.fold_in(_rk, 2), 23), (512,), 4, 199965, jnp.int32), jax.random.randint(jax.random.fold_in(jax.random.fold_in(_rk, 2), 24), (512,), 6, 199998, jnp.int32), jax.random.randint(jax.random.fold_in(jax.random.fold_in(_rk, 2), 25), (512,), 2, 199972, jnp.int32)], axis=1)
        return (r_num, r_cat)
    r_num, r_cat = _rec_inputs()

    def _L0_rec_setup():
        import jax, jax.numpy as jnp
        import numpy as np
        B = 1024
        NUM = 256
        F = 26
        V = 25000
        E = 64
        P = 128
        BOT = [NUM, 512, 256, 128]
        N = F + 1
        _TRIU = np.triu_indices(N, k=1)
        INTER = len(_TRIU[0])
        TOP = [NUM + INTER, 512, 256, 1]

        def _leaky(x):
            return jnp.where(x > 0, x, 0.01 * x)

        def _mlp_params(key, dims, scale=0.02):
            out = []
            for i, (a, b) in enumerate(zip(dims[:-1], dims[1:])):
                k = jax.random.fold_in(key, i)
                out.append((jax.random.normal(k, (a, b), dtype=jnp.float32) * scale, jnp.zeros((b,), dtype=jnp.float32)))
            return out

        def _forward(num, cat, tables, proj_w, proj_b, bot, top):
            x = num
            for w, b in bot:
                x = _leaky(x @ w + b)
            emb = jax.vmap(lambda t, i: t[i], in_axes=(0, 1))(tables, cat)
            sp = jnp.einsum('fbe,fep->fbp', emb, proj_w) + proj_b[:, None, :]
            feats = jnp.concatenate([x[None], sp], axis=0).transpose(1, 0, 2)
            dots = jnp.einsum('bne,bme->bnm', feats, feats)
            inter = dots[:, _TRIU[0], _TRIU[1]]
            out = jnp.concatenate([inter, num], axis=1)
            for w, b in top[:-1]:
                out = _leaky(out @ w + b)
            w, b = top[-1]
            out = jax.nn.sigmoid(out @ w + b)
            return out.squeeze(1)
        key = jax.random.key(seed)
        k = jax.random.split(key, 6)
        num = jax.random.normal(k[0], (B, NUM), dtype=jnp.float32)
        cat = jax.random.randint(k[1], (B, F), 0, V)
        tables = jax.random.normal(k[2], (F, V, E), dtype=jnp.float32) * 0.02
        proj_w = jax.random.normal(k[3], (F, E, P), dtype=jnp.float32) * 0.02
        proj_b = jnp.zeros((F, P), dtype=jnp.float32)
        bot = _mlp_params(k[4], BOT)
        top = _mlp_params(k[5], TOP)
        d = dict(num=num, cat=cat, tables=tables, proj_w=proj_w, proj_b=proj_b)
        for i, (w, b) in enumerate(bot):
            d[f'bot_w{i}'] = w
            d[f'bot_b{i}'] = b
        for i, (w, b) in enumerate(top):
            d[f'top_w{i}'] = w
            d[f'top_b{i}'] = b
        return d
    _L0_rec_all = _L0_rec_setup()
    _L0_rec_in = {k: v for k, v in _L0_rec_all.items() if k in ('tables', 'proj_w', 'proj_b', 'bot_w0', 'bot_b0', 'bot_w1', 'bot_b1', 'bot_w2', 'bot_b2', 'top_w0', 'top_b0', 'top_w1', 'top_b1', 'top_w2', 'top_b2')}
    del _L0_rec_all
    return {'r_num': r_num, 'r_cat': r_cat, 'L0_rec_tables': _L0_rec_in['tables'], 'L0_rec_proj_w': _L0_rec_in['proj_w'], 'L0_rec_proj_b': _L0_rec_in['proj_b'], 'L0_rec_bot_w0': _L0_rec_in['bot_w0'], 'L0_rec_bot_b0': _L0_rec_in['bot_b0'], 'L0_rec_bot_w1': _L0_rec_in['bot_w1'], 'L0_rec_bot_b1': _L0_rec_in['bot_b1'], 'L0_rec_bot_w2': _L0_rec_in['bot_w2'], 'L0_rec_bot_b2': _L0_rec_in['bot_b2'], 'L0_rec_top_w0': _L0_rec_in['top_w0'], 'L0_rec_top_b0': _L0_rec_in['top_b0'], 'L0_rec_top_w1': _L0_rec_in['top_w1'], 'L0_rec_top_b1': _L0_rec_in['top_b1'], 'L0_rec_top_w2': _L0_rec_in['top_w2'], 'L0_rec_top_b2': _L0_rec_in['top_b2']}

def reference(r_num, r_cat, L0_rec_tables, L0_rec_proj_w, L0_rec_proj_b, L0_rec_bot_w0, L0_rec_bot_b0, L0_rec_bot_w1, L0_rec_bot_b1, L0_rec_bot_w2, L0_rec_bot_b2, L0_rec_top_w0, L0_rec_top_b0, L0_rec_top_w1, L0_rec_top_b1, L0_rec_top_w2, L0_rec_top_b2):
    import jax
    import jax.numpy as jnp

    def _L0_rec_ref(num, cat, tables, proj_w, proj_b, bot_w0, bot_b0, bot_w1, bot_b1, bot_w2, bot_b2, top_w0, top_b0, top_w1, top_b1, top_w2, top_b2):
        import jax, jax.numpy as jnp
        import numpy as np
        B = 1024
        NUM = 256
        F = 26
        V = 25000
        E = 64
        P = 128
        BOT = [NUM, 512, 256, 128]
        N = F + 1
        _TRIU = np.triu_indices(N, k=1)
        INTER = len(_TRIU[0])
        TOP = [NUM + INTER, 512, 256, 1]

        def _leaky(x):
            return jnp.where(x > 0, x, 0.01 * x)

        def _mlp_params(key, dims, scale=0.02):
            out = []
            for i, (a, b) in enumerate(zip(dims[:-1], dims[1:])):
                k = jax.random.fold_in(key, i)
                out.append((jax.random.normal(k, (a, b), dtype=jnp.float32) * scale, jnp.zeros((b,), dtype=jnp.float32)))
            return out

        def _forward(num, cat, tables, proj_w, proj_b, bot, top):
            x = num
            for w, b in bot:
                x = _leaky(x @ w + b)
            emb = jax.vmap(lambda t, i: t[i], in_axes=(0, 1))(tables, cat)
            sp = jnp.einsum('fbe,fep->fbp', emb, proj_w) + proj_b[:, None, :]
            feats = jnp.concatenate([x[None], sp], axis=0).transpose(1, 0, 2)
            dots = jnp.einsum('bne,bme->bnm', feats, feats)
            inter = dots[:, _TRIU[0], _TRIU[1]]
            out = jnp.concatenate([inter, num], axis=1)
            for w, b in top[:-1]:
                out = _leaky(out @ w + b)
            w, b = top[-1]
            out = jax.nn.sigmoid(out @ w + b)
            return out.squeeze(1)
        bot = [(bot_w0, bot_b0), (bot_w1, bot_b1), (bot_w2, bot_b2)]
        top = [(top_w0, top_b0), (top_w1, top_b1), (top_w2, top_b2)]
        return _forward(num, cat, tables, proj_w, proj_b, bot, top)
    y = _L0_rec_ref(r_num, r_cat, L0_rec_tables, L0_rec_proj_w, L0_rec_proj_b, L0_rec_bot_w0, L0_rec_bot_b0, L0_rec_bot_w1, L0_rec_bot_b1, L0_rec_bot_w2, L0_rec_bot_b2, L0_rec_top_w0, L0_rec_top_b0, L0_rec_top_w1, L0_rec_top_b1, L0_rec_top_w2, L0_rec_top_b2)
    return y

_drawn_inputs = setup_inputs


def setup_inputs(seed=0):
    import zlib

    import numpy as np

    out = dict(_drawn_inputs(seed))
    spreads = {'L0_rec_proj_b': (0.0, 0.8),
     'L0_rec_bot_b0': (0.0, 0.8),
     'L0_rec_bot_b1': (0.0, 0.8),
     'L0_rec_bot_b2': (0.0, 0.8),
     'L0_rec_top_b0': (0.0, 2.0),
     'L0_rec_top_b1': (0.0, 2.0)}
    factors = {'r_num': 6.123,
     'L0_rec_tables': 8.0,
     'L0_rec_proj_w': 8.0,
     'L0_rec_bot_w0': 8.0,
     'L0_rec_bot_w1': 8.0,
     'L0_rec_bot_w2': 8.0,
     'L0_rec_top_w0': 5.958,
     'L0_rec_top_w1': 5.481,
     'L0_rec_top_w2': 3.76}
    for name, (base, spread) in spreads.items():
        noise = np.random.default_rng([zlib.crc32(name.encode()), seed]).standard_normal(out[name].shape)
        drawn = base * np.exp(spread * noise) if base else spread * noise
        out[name] = jnp.asarray(drawn.astype(out[name].dtype))
    for name, factor in factors.items():
        out[name] = (out[name] * factor).astype(out[name].dtype)
    return out
```

```python
import concourse.bass as bass
from concourse import mybir
from contextlib import ExitStack


def recommender_kernel(
    nc: bass.Bass,
    r_num: bass.AP,
    r_cat: bass.AP,
    tables: bass.AP,
    proj_w: bass.AP,
    proj_b: bass.AP,
    bot_w0: bass.AP,
    bot_b0: bass.AP,
    bot_w1: bass.AP,
    bot_b1: bass.AP,
    bot_w2: bass.AP,
    bot_b2: bass.AP,
    top_w0: bass.AP,
    top_b0: bass.AP,
    top_w1: bass.AP,
    top_b1: bass.AP,
    top_w2: bass.AP,
    top_b2: bass.AP,
    pair_rows: bass.AP,
    scratch: bass.AP,
    out: bass.AP,
):
    fp32 = mybir.dt.float32
    i32 = mybir.dt.int32
    u32 = mybir.dt.uint32
    ALU = mybir.AluOpType
    ACT = mybir.ActivationFunctionType

    P = 128
    BATCH, NUM = r_num.shape
    NF, VOCAB, EMB = tables.shape
    TILES = BATCH // P
    PAIRS = NF // 2
    FEATS = NF + 1
    SLOTS = 32
    QUAD = P // SLOTS
    QUADS = P // QUAD
    GROUP = 8
    GROUPS = QUADS // GROUP
    PER_BANK = 4
    INTER = FEATS * (FEATS - 1) // 2
    DIST = (FEATS - 1) // 2
    NPC = 9
    CHUNKS = FEATS // NPC
    ROWS = NPC * DIST
    WIDE = FEATS + DIST
    NUMC = NUM // P
    H0, H1, H2 = bot_w0.shape[1], bot_w1.shape[1], bot_w2.shape[1]
    G0, G1 = top_w0.shape[1], top_w1.shape[1]
    LEAK = 0.01

    table_rows = tables.rearrange("f v e -> (f v) e")

    with ExitStack() as ctx:
        def sb(name, shape, dt=fp32):
            return ctx.enter_context(nc.sbuf_tensor(name, shape, dt))

        def pb(name, shape):
            return ctx.enter_context(nc.psum_tensor(name, shape, fp32))

        def sem(name):
            return ctx.enter_context(nc.semaphore(name))

        cat = sb("cat", [P, TILES, NF], i32)
        first_row = sb("first_row", [P, NF], i32)
        wrap = sb("wrap", [P, TILES, NF])
        wrapped = sb("wrapped", [P, TILES, NF])
        clamped = sb("clamped", [P, TILES, NF])
        index = sb("index", [P, TILES, NF], i32)
        ident = sb("ident", [P, P])
        num = sb("num", [P, TILES, NUM])
        numT = sb("numT", [P, NUMC, BATCH])
        wp = sb("wp", [P, NF, P])
        pbias = sb("pbias", [P, NF])
        wb0 = sb("wb0", [P, NUMC, H0])
        wb1 = sb("wb1", [P, H0 // P, H1])
        wb2 = sb("wb2", [P, H1 // P, H2])
        bb0 = sb("bb0", [P, H0 // P])
        bb1 = sb("bb1", [P, H1 // P])
        bb2 = sb("bb2", [P, H2 // P])
        pair_row = sb("pair_row", [ROWS, CHUNKS], i32)
        wt0 = sb("wt0", [ROWS, CHUNKS, G0])
        wt0n = sb("wt0n", [P, NUMC, G0])
        wt1 = sb("wt1", [P, G0 // P, G1])
        wt2 = sb("wt2", [P, G1 // P])
        bt0 = sb("bt0", [P, G0 // P])
        bt1 = sb("bt1", [P, G1 // P])
        bt2 = sb("bt2", [1, 1])
        hb0 = sb("hb0", [P, H0 // P, BATCH])
        hb1 = sb("hb1", [P, H1 // P, BATCH])
        xbot = sb("xbot", [P, BATCH])
        emb = sb("emb", [P, NF, EMB])
        embT = sb("embT", [P, 2, P])
        feats = [sb(f"feats{i}", [P, P, SLOTS]) for i in range(2)]
        dots = sb("dots", [SLOTS, FEATS, P])
        inter = sb("inter", [ROWS, CHUNKS, P])
        ht0 = sb("ht0", [P, G0 // P, P])
        ht1 = sb("ht1", [P, G1 // P, P])
        bot_pre = sb("bot_pre", [P, 2, BATCH])
        top0_pre = sb("top0_pre", [P, G0 // P, P])
        top1_pre = sb("top1_pre", [P, G1 // P, P])
        score = sb("score", [1, BATCH])

        ps_t = pb("ps_t", [P, 4, P])[:, 0, :]
        ps_p = pb("ps_p", [P, 4, P])[:, 0:2, :]
        ps_g = [pb(f"ps_g{i}", [P, GROUP, P]) for i in range(2)]
        ps_h = [pb(f"ps_h{i}", [P, 512]) for i in range(2)]

        cat_loaded = sem("cat_loaded")
        first_ready = sem("first_ready")
        index_step = sem("index_step")
        index_ready = sem("index_ready")
        num_loaded = sem("num_loaded")
        bot0_loaded = sem("bot0_loaded")
        bot1_loaded = sem("bot1_loaded")
        bot2_loaded = sem("bot2_loaded")
        proj_loaded = sem("proj_loaded")
        top0_loaded = sem("top0_loaded")
        pair_weights_loaded = sem("pair_weights_loaded")
        top1_loaded = sem("top1_loaded")
        ident_zeroed = sem("ident_zeroed")
        ident_ready = sem("ident_ready")
        padded = sem("padded")
        gathered = [sem(f"gathered{j}") for j in range(PAIRS)]
        num_transposed = sem("num_transposed")
        num_placed = sem("num_placed")
        hidden_done = sem("hidden_done")
        hidden_read = sem("hidden_read")
        bot_placed = sem("bot_placed")
        emb_transposed = sem("emb_transposed")
        emb_placed = sem("emb_placed")
        projected = sem("projected")
        feats_placed = sem("feats_placed")
        x_placed = sem("x_placed")
        dots_done = sem("dots_done")
        dots_by_dve = sem("dots_by_dve")
        dots_by_act = sem("dots_by_act")
        pairs_loaded = sem("pairs_loaded")
        dots_written = sem("dots_written")
        relaid = sem("relaid")
        top0_placed = sem("top0_placed")
        top1_placed = sem("top1_placed")
        stored = sem("stored")

        BOT = (H0 + H1 + H2) // P
        TOP0, TOP1 = G0 // P, G1 // P
        TOP = TOP0 + TOP1 + 1

        def top_block(t, i):
            return BOT + TOP * t + i

        block = ctx.enter_context(nc.Block())

        def by_sample(t):
            return feats[t % 2][:].rearrange("p (q g) n -> p g q n", g=QUAD)

        def dots_block(t, group, g):
            src = ps_g[group % 2][SLOTS * g:SLOTS * g + SLOTS, :, FEATS * g:FEATS * g + FEATS]
            q0 = QUADS * g + GROUP * group
            return dots[:, :, q0:q0 + GROUP], src.rearrange("n q m -> n m q")

        by_feature = scratch[0:FEATS * WIDE * P].rearrange("(n m b) -> n m b", n=FEATS, b=P)
        by_distance = scratch.rearrange("(n d b) -> n d b", n=FEATS, b=P)

        @block.sync
        def _(sp):
            sp.dma_start(cat[:], r_cat.rearrange("(t p) f -> p t f", p=P)).then_inc(cat_loaded, 16)
            sp.dma_start(pair_row[:], pair_rows).then_inc(pairs_loaded, 16)
            sp.dma_start(num[:], r_num.rearrange("(t p) c -> p t c", p=P)).then_inc(num_loaded, 16)
            sp.dma_start(bb0[:], bot_b0.rearrange("(c p) -> p c", p=P),
                         allow_slow_non_contiguous=True).then_inc(bot0_loaded, 16)
            even_odd = proj_w.rearrange("(j two) e p -> two e j p", two=2)
            wp_pairs = wp[:].rearrange("q (j two) p -> q j two p", two=2)
            for half in range(2):
                sp.dma_start(wp_pairs[EMB * half:EMB * half + EMB, :, half, :],
                             even_odd[half]).then_inc(proj_loaded, 16)
            sp.dma_start(pbias[:], proj_b.rearrange("f p -> p f"),
                         allow_slow_non_contiguous=True).then_inc(proj_loaded, 16)
            sp.dma_start(wb2[:], bot_w2.rearrange("(c p) h -> p c h", p=P)).then_inc(bot2_loaded, 16)
            sp.dma_start(bb2[:], bot_b2.rearrange("(c p) -> p c", p=P),
                         allow_slow_non_contiguous=True).then_inc(bot2_loaded, 16)
            sp.dma_start(wt0n[:], top_w0[INTER:INTER + NUM, :].rearrange("(c p) h -> p c h", p=P)
                         ).then_inc(top0_loaded, 16)
            sp.dma_start(bt0[:], top_b0.rearrange("(c p) -> p c", p=P),
                         allow_slow_non_contiguous=True).then_inc(top0_loaded, 16)
            sp.dma_start(wt1[:], top_w1.rearrange("(c p) h -> p c h", p=P)).then_inc(top1_loaded, 16)
            sp.dma_start(bt1[:], top_b1.rearrange("(c p) -> p c", p=P),
                         allow_slow_non_contiguous=True).then_inc(top1_loaded, 16)
            sp.dma_start(wt2[:], top_w2.rearrange("(c p) h -> p (c h)", p=P),
                         allow_slow_non_contiguous=True).then_inc(top1_loaded, 16)
            sp.dma_start(bt2[:], top_b2.rearrange("(p c) -> p c", p=1)).then_inc(top1_loaded, 16)
            for t in range(TILES):
                sp.wait_ge(dots_by_dve, 2 * GROUPS * (t + 1))
                sp.wait_ge(dots_by_act, 2 * GROUPS * (t + 1))
                if t > 0:
                    sp.wait_ge(relaid, 16 * CHUNKS * t)
                sp.dma_start(by_feature[:, 0:FEATS, :], dots[0:FEATS]).then_inc(dots_written, 16)
                sp.dma_start(by_feature[:, FEATS:WIDE, :], dots[0:FEATS, 0:DIST, :]).then_inc(dots_written, 16)
                sp.wait_ge(dots_written, 32 * (t + 1))
                if t > 0:
                    sp.wait_ge(hidden_done, top_block(t - 1, TOP0))
                for c in range(CHUNKS):
                    sp.dma_start(inter[:, c, :], by_distance[NPC * c:NPC * c + NPC, 1:DIST + 1, :]
                                 ).then_inc(relaid, 16)
            sp.wait_ge(hidden_read, top_block(TILES, 0))
            sp.dma_start(out.rearrange("(o b) -> o b", o=1), score[:]).then_inc(stored, 16)
            sp.wait_ge(stored, 16)

        @block.gpsimd
        def _(pool):
            nc.gpsimd.iota(first_row[:], [[VOCAB, NF]], base=0, channel_multiplier=0).then_inc(first_ready, 1)
            nc.gpsimd.memset(ident[:], 0.0).then_inc(ident_zeroed, 1)
            pool.wait_ge(ident_zeroed, 1)
            nc.gpsimd.affine_select(out=ident[:], in_=ident[:], compare_op=ALU.not_equal, fill=1.0, base=0,
                                    pattern=[[-1, P]], channel_multiplier=1).then_inc(ident_ready, 1)
            pool.wait_ge(pairs_loaded, 16)
            for c in range(CHUNKS):
                nc.gpsimd.indirect_dma_start(
                    wt0[:, c, :], None, top_w0,
                    bass.IndirectOffsetOnAxis(ap=pair_row[:, c:c + 1].bitcast(u32), axis=0),
                ).then_inc(pair_weights_loaded, 16)
            pool.wait_ge(index_ready, 1)
            for t in range(TILES):
                for f in range(NF):
                    if t > 0 and f % 2 == 0:
                        pool.wait_ge(emb_transposed, PAIRS * (t - 1) + f // 2 + 1)
                    nc.gpsimd.indirect_dma_start(
                        emb[:, f, :], None, table_rows,
                        bass.IndirectOffsetOnAxis(ap=index[:, t, f:f + 1].bitcast(u32), axis=0),
                    ).then_inc(gathered[f // 2], 16)

        @block.scalar
        def _(act):
            act.dma_start(wb0[:], bot_w0.rearrange("(c p) h -> p c h", p=P)).then_inc(bot0_loaded, 16)
            act.dma_start(wb1[:], bot_w1.rearrange("(c p) h -> p c h", p=P)).then_inc(bot1_loaded, 16)
            act.dma_start(bb1[:], bot_b1.rearrange("(c p) -> p c", p=P),
                          allow_slow_non_contiguous=True).then_inc(bot1_loaded, 16)

            def add_bias(dst, src, bias):
                return nc.scalar.activation(dst, src, ACT.Identity, bias=bias)

            def bottom(i, bias):
                act.wait_ge(hidden_done, i + 1)
                if i >= 2:
                    act.wait_ge(bot_placed, i - 1)
                add_bias(bot_pre[:, i % 2, :], ps_h[i % 2][:], bias).then_inc(hidden_read, 1)

            def place_x(t):
                if t >= 2:
                    act.wait_ge(dots_done, GROUPS * (t - 1))
                nc.scalar.copy(by_sample(t)[:, :, :, 0],
                               xbot[:, P * t:P * t + P].rearrange("p (g q) -> p g q", g=QUAD)).then_inc(x_placed, 1)

            def place_emb(k):
                act.wait_ge(emb_transposed, k + 1)
                if k >= 2:
                    act.wait_ge(projected, k - 1)
                nc.scalar.copy(embT[:, k % 2, :], ps_t).then_inc(emb_placed, 1)

            def place_dots(t, group):
                act.wait_ge(dots_done, GROUPS * t + group + 1)
                if group == 0 and t > 0:
                    act.wait_ge(dots_written, 32 * t)
                for g in (2, 3):
                    dst, src = dots_block(t, group, g)
                    nc.scalar.copy(dst, src).then_inc(dots_by_act, 1)

            def top0(t):
                if t > 0:
                    act.wait_ge(top0_placed, TOP0 * t)
                for h in range(TOP0):
                    i = top_block(t, h)
                    act.wait_ge(hidden_done, i + 1)
                    add_bias(top0_pre[:, h, :], ps_h[i % 2][:, 0:P], bt0[:, h:h + 1]).then_inc(hidden_read, 1)

            def top1(t):
                if t > 0:
                    act.wait_ge(top1_placed, TOP1 * t)
                for h in range(TOP1):
                    i = top_block(t, TOP0 + h)
                    act.wait_ge(hidden_done, i + 1)
                    add_bias(top1_pre[:, h, :], ps_h[i % 2][:, 0:P], bt1[:, h:h + 1]).then_inc(hidden_read, 1)

            def top2(t):
                i = top_block(t, TOP0 + TOP1)
                act.wait_ge(hidden_done, i + 1)
                nc.scalar.activation(score[0:1, P * t:P * t + P], ps_h[i % 2][0:1, 0:P], ACT.Sigmoid,
                                     bias=bt2[:]).then_inc(hidden_read, 1)

            act.wait_ge(bot0_loaded, 32)
            for h in range(H0 // P):
                bottom(h, bb0[:, h:h + 1])
            for t in range(TILES):
                if t > 0:
                    place_x(t)
                for j in range(PAIRS):
                    place_emb(PAIRS * t + j)
                    if t == 0:
                        if j == 1:
                            act.wait_ge(bot1_loaded, 32)
                        if j in (2, 4):
                            h = j // 2 - 1
                            bottom(H0 // P + h, bb1[:, h:h + 1])
                        if j == 5:
                            act.wait_ge(bot2_loaded, 32)
                            bottom(H0 // P + H1 // P, bb2[:])
                            act.wait_ge(bot_placed, H0 // P + H1 // P + 1)
                            place_x(0)
                            act.wait_ge(top0_loaded, 32)
                            act.wait_ge(top1_loaded, 64)
                    else:
                        if j < 2 * GROUPS and j % 2 == 1:
                            place_dots(t - 1, j // 2)
                        if j == 11:
                            top0(t - 1)
                        if j == 12:
                            top1(t - 1)
                            top2(t - 1)
            for group in range(GROUPS):
                place_dots(TILES - 1, group)
            top0(TILES - 1)
            top1(TILES - 1)
            top2(TILES - 1)

        @block.vector
        def _(dve):
            dve.wait_ge(cat_loaded, 16)
            nc.vector.tensor_scalar(wrap[:], cat[:], 0.0, float(VOCAB), ALU.is_lt, ALU.mult).then_inc(index_step, 1)
            dve.wait_ge(index_step, 1)
            nc.vector.tensor_tensor(wrapped[:], wrap[:], cat[:], ALU.add).then_inc(index_step, 1)
            dve.wait_ge(index_step, 2)
            nc.vector.tensor_scalar(clamped[:], wrapped[:], float(VOCAB - 1), 0.0, ALU.min, ALU.max
                                    ).then_inc(index_step, 1)
            dve.wait_ge(index_step, 3)
            dve.wait_ge(first_ready, 1)
            nc.vector.tensor_tensor(index[:], clamped[:], first_row[:].unsqueeze(1).broadcast_to([P, TILES, NF]),
                                    ALU.add).then_inc(index_ready, 1)
            wp_pairs = wp[:].rearrange("q (j two) p -> q j two p", two=2)
            nc.vector.memset(wp_pairs[EMB:P, :, 0, :], 0.0)
            nc.vector.memset(wp_pairs[0:EMB, :, 1, :], 0.0)
            for buf in feats:
                last = nc.vector.memset(buf[:, :, FEATS:SLOTS], 0.0)
            last.then_inc(padded, 1)

            for c in range(NUMC):
                dve.wait_ge(num_transposed, c + 1)
                nc.vector.tensor_copy(numT[:, c, :], ps_g[0][:].rearrange("p q b -> p (q b)")[
                    :, BATCH * c:BATCH * c + BATCH]).then_inc(num_placed, 1)

            def place_feats(k):
                t, j = k // PAIRS, k % PAIRS
                dve.wait_ge(projected, k + 1)
                if t >= 2 and j == 0:
                    dve.wait_ge(dots_done, GROUPS * (t - 1))
                nc.vector.tensor_tensor(
                    by_sample(t)[:, :, :, 2 * j + 1:2 * j + 3],
                    ps_p.rearrange("p f (g q) -> p g q f", g=QUAD),
                    pbias[:, 2 * j:2 * j + 2].unsqueeze(1).unsqueeze(1).broadcast_to([P, QUAD, QUADS, 2]),
                    ALU.add).then_inc(feats_placed, 1)

            def place_dots(t, group):
                dve.wait_ge(dots_done, GROUPS * t + group + 1)
                if group == 0 and t > 0:
                    dve.wait_ge(dots_written, 32 * t)
                for g in (0, 1):
                    dst, src = dots_block(t, group, g)
                    nc.vector.tensor_copy(dst, src).then_inc(dots_by_dve, 1)

            def leaky(dst, pre):
                return nc.vector.scalar_tensor_tensor(out=dst, in0=pre, scalar=LEAK, in1=pre,
                                                      op0=ALU.mult, op1=ALU.max)

            def bottom(i, dst):
                dve.wait_ge(hidden_read, i + 1)
                leaky(dst, bot_pre[:, i % 2, :]).then_inc(bot_placed, 1)

            def top0(t):
                if t > 0:
                    dve.wait_ge(hidden_done, top_block(t - 1, TOP0 + TOP1))
                for h in range(TOP0):
                    dve.wait_ge(hidden_read, top_block(t, h) + 1)
                    leaky(ht0[:, h, :], top0_pre[:, h, :]).then_inc(top0_placed, 1)

            def top1(t):
                if t > 0:
                    dve.wait_ge(hidden_done, top_block(t, 0))
                for h in range(TOP1):
                    dve.wait_ge(hidden_read, top_block(t, TOP0 + h) + 1)
                    leaky(ht1[:, h, :], top1_pre[:, h, :]).then_inc(top1_placed, 1)

            for h in range(H0 // P):
                bottom(h, hb0[:, h, :])
            dve.wait_ge(proj_loaded, 48)
            for t in range(TILES):
                for j in range(PAIRS):
                    k = PAIRS * t + j
                    if k > 0:
                        place_feats(k - 1)
                    if t == 0:
                        if j in (2, 4):
                            h = j // 2 - 1
                            bottom(H0 // P + h, hb1[:, h, :])
                        if j == 5:
                            bottom(H0 // P + H1 // P, xbot[:])
                    else:
                        if j < 2 * GROUPS and j % 2 == 1:
                            place_dots(t - 1, j // 2)
                        if j == 11:
                            top0(t - 1)
                        if j == 12:
                            top1(t - 1)
            place_feats(PAIRS * TILES - 1)
            for group in range(GROUPS):
                place_dots(TILES - 1, group)
            top0(TILES - 1)
            top1(TILES - 1)

        @block.tensor
        def _(pe):
            def transpose_pair(k):
                t, j = k // PAIRS, k % PAIRS
                pe.wait_ge(gathered[j], 32 * (t + 1))
                if k > 0:
                    pe.wait_ge(emb_placed, k)
                nc.tensor.transpose(ps_t, emb[:, 2 * j:2 * j + 2, :].rearrange("p f e -> p (f e)"),
                                    ident[:]).then_inc(emb_transposed, 1)

            def project_pair(k):
                j = k % PAIRS
                pe.wait_ge(emb_placed, k + 1)
                if k > 0:
                    pe.wait_ge(feats_placed, k)
                for f in range(2):
                    last = nc.tensor.matmul(ps_p[:, f, :], wp[:, 2 * j + f, :], embT[:, k % 2, :],
                                            start=True, stop=True)
                last.then_inc(projected, 1)

            def free_bank(i):
                if i >= 2:
                    pe.wait_ge(hidden_read, i - 1)

            def bottom(i, w, h, x, start, stop):
                chunks = w.shape[1]
                for c in range(start, stop):
                    last = nc.tensor.matmul(ps_h[i % 2][:], w[:, c, P * h:P * h + P], x[:, c, :],
                                            start=(c == 0), stop=(c == chunks - 1))
                if stop == chunks:
                    last.then_inc(hidden_done, 1)

            def dot_quads(t, lo, hi):
                buf = feats[t % 2]
                if lo == 0:
                    pe.wait_ge(feats_placed, PAIRS * (t + 1))
                    pe.wait_ge(x_placed, t + 1)
                for q in range(lo, hi):
                    group = q // GROUP
                    if q % GROUP == 0 and GROUPS * t + group >= 2:
                        pe.wait_ge(dots_by_dve, 2 * (GROUPS * t + group - 1))
                        pe.wait_ge(dots_by_act, 2 * (GROUPS * t + group - 1))
                    four = buf[:, QUAD * q:QUAD * q + QUAD, :]
                    last = nc.tensor.matmul(ps_g[group % 2][:, q % GROUP, 0:QUAD * FEATS],
                                            four.rearrange("p g n -> p (g n)"), four[:, :, 0:FEATS],
                                            start=True, stop=True)
                    if q % GROUP == GROUP - 1:
                        last.then_inc(dots_done, 1)

            def top0(t):
                for h in range(TOP0):
                    i = top_block(t, h)
                    cols = slice(P * h, P * h + P)
                    free_bank(i)
                    for c in range(NUMC):
                        nc.tensor.matmul(ps_h[i % 2][:, 0:P], wt0n[:, c, cols], numT[:, c, P * t:P * t + P],
                                         start=(c == 0), stop=False)
                    if h == 0:
                        pe.wait_ge(relaid, 16 * CHUNKS * (t + 1))
                    for c in range(CHUNKS):
                        last = nc.tensor.matmul(ps_h[i % 2][:, 0:P], wt0[:, c, cols], inter[:, c, :],
                                                start=False, stop=(c == CHUNKS - 1))
                    last.then_inc(hidden_done, 1)

            def top1(t):
                for h in range(TOP1):
                    i = top_block(t, TOP0 + h)
                    cols = slice(P * h, P * h + P)
                    free_bank(i)
                    for c in range(TOP0):
                        if h == 0:
                            pe.wait_ge(top0_placed, TOP0 * t + c + 1)
                        last = nc.tensor.matmul(ps_h[i % 2][:, 0:P], wt1[:, c, cols], ht0[:, c, :],
                                                start=(c == 0), stop=(c == TOP0 - 1))
                    last.then_inc(hidden_done, 1)

            def top2(t):
                i = top_block(t, TOP0 + TOP1)
                free_bank(i)
                for c in range(TOP1):
                    pe.wait_ge(top1_placed, TOP1 * t + c + 1)
                    last = nc.tensor.matmul(ps_h[i % 2][0:1, 0:P], wt2[:, c:c + 1], ht1[:, c, :],
                                            start=(c == 0), stop=(c == TOP1 - 1))
                last.then_inc(hidden_done, 1)

            pe.wait_ge(ident_ready, 1)
            pe.wait_ge(num_loaded, 16)
            flat_g = ps_g[0][:].rearrange("p q b -> p (q b)")
            for c in range(NUMC):
                for t in range(TILES):
                    col = BATCH * c + P * t
                    last = nc.tensor.transpose(flat_g[:, col:col + P], num[:, t, P * c:P * c + P], ident[:])
                last.then_inc(num_transposed, 1)
            pe.wait_ge(num_placed, NUMC)
            pe.wait_ge(bot0_loaded, 32)
            for h in range(H0 // P):
                free_bank(h)
                bottom(h, wb0, h, numT, 0, NUMC)
            for t in range(TILES):
                for j in range(PAIRS):
                    k = PAIRS * t + j
                    transpose_pair(k)
                    if k == 1:
                        pe.wait_ge(proj_loaded, 48)
                        pe.wait_ge(padded, 1)
                    if k > 0:
                        project_pair(k - 1)
                    if t == 0:
                        if j == 1:
                            pe.wait_ge(bot1_loaded, 32)
                            pe.wait_ge(bot_placed, H0 // P)
                        if 1 <= j <= 4:
                            h, half = (j - 1) // 2, (j - 1) % 2
                            if half == 0:
                                free_bank(H0 // P + h)
                            bottom(H0 // P + h, wb1, h, hb0, 2 * half, 2 * half + 2)
                        if j == 5:
                            pe.wait_ge(bot2_loaded, 32)
                            pe.wait_ge(bot_placed, H0 // P + H1 // P)
                            free_bank(H0 // P + H1 // P)
                            bottom(H0 // P + H1 // P, wb2, 0, hb1, 0, H1 // P)
                            pe.wait_ge(pair_weights_loaded, 16 * CHUNKS)
                            pe.wait_ge(top0_loaded, 32)
                            pe.wait_ge(top1_loaded, 64)
                    else:
                        if j < 2 * GROUPS:
                            dot_quads(t - 1, 4 * j, 4 * j + 4)
                        if j == 11:
                            top0(t - 1)
                        if j == 12:
                            top1(t - 1)
                            top2(t - 1)
            project_pair(PAIRS * TILES - 1)
            dot_quads(TILES - 1, 0, QUADS)
            top0(TILES - 1)
            top1(TILES - 1)
            top2(TILES - 1)


_INS = ["r_num", "r_cat", "L0_rec_tables", "L0_rec_proj_w", "L0_rec_proj_b",
        "L0_rec_bot_w0", "L0_rec_bot_b0", "L0_rec_bot_w1", "L0_rec_bot_b1", "L0_rec_bot_w2", "L0_rec_bot_b2",
        "L0_rec_top_w0", "L0_rec_top_b0", "L0_rec_top_w1", "L0_rec_top_b1", "L0_rec_top_w2", "L0_rec_top_b2"]


def kernel(**inputs):
    import numpy as _np
    import concourse.bacc as _bacc
    from concourse import mybir as _mybir
    from concourse.bass_utils import run_bass_kernel_spmd as _run

    nc = _bacc.Bacc("TRN2", target_bir_lowering=False, num_devices=1)
    arrays, args = {}, []
    for name in _INS:
        a = _np.ascontiguousarray(inputs[name])
        arrays[f"in_{name}_dram"] = a
        args.append(nc.dram_tensor(f"in_{name}_dram", a.shape, _mybir.dt.from_np(a.dtype), kind="ExternalInput").ap())
    feats = arrays["in_L0_rec_tables_dram"].shape[0] + 1
    dist, chunks, part = (feats - 1) // 2, feats // 9, 128
    row = {}
    for n in range(feats):
        for m in range(n + 1, feats):
            row[n, m] = row[m, n] = len(row) // 2
    rows = _np.array([[row[n, (n + d) % feats] for d in range(1, dist + 1)] for n in range(feats)], _np.int32)
    arrays["in_pair_rows_dram"] = _np.ascontiguousarray(rows.reshape(chunks, 9 * dist).T)
    args.append(nc.dram_tensor("in_pair_rows_dram", (9 * dist, chunks), _mybir.dt.int32, kind="ExternalInput").ap())
    args.append(nc.dram_tensor("scratch_dram", (feats * (feats + dist + 1) * part,), _mybir.dt.float32,
                               kind="Internal").ap())
    batch = arrays["in_r_num_dram"].shape[0]
    args.append(nc.dram_tensor("out_0_dram", (batch,), _mybir.dt.float32, kind="ExternalOutput").ap())
    recommender_kernel(nc, *args)
    r = _run(nc, [arrays], core_ids=[0])
    return r.results[0]["out_0_dram"]
```

```python
import concourse.bass as bass
from concourse import mybir
from contextlib import ExitStack


def recommender_kernel(
    nc: bass.Bass,
    r_num: bass.AP,
    r_cat: bass.AP,
    tables: bass.AP,
    proj_w: bass.AP,
    proj_b: bass.AP,
    bot_w0: bass.AP,
    bot_b0: bass.AP,
    bot_w1: bass.AP,
    bot_b1: bass.AP,
    bot_w2: bass.AP,
    bot_b2: bass.AP,
    top_w0: bass.AP,
    top_b0: bass.AP,
    top_w1: bass.AP,
    top_b1: bass.AP,
    top_w2: bass.AP,
    top_b2: bass.AP,
    scratch: bass.AP,
    out: bass.AP,
):
    fp32 = mybir.dt.float32
    i32 = mybir.dt.int32
    u32 = mybir.dt.uint32
    ALU = mybir.AluOpType
    ACT = mybir.ActivationFunctionType

    P = 128
    BATCH, NUM = r_num.shape
    NF, VOCAB, EMB = tables.shape
    TILES = BATCH // P
    PAIRS = NF // 2
    FEATS = NF + 1
    SLOTS = 32
    QUAD = P // SLOTS
    QUADS = P // QUAD
    GROUP = 4
    GROUPS = QUADS // GROUP
    BANKS = 3
    INTER = FEATS * (FEATS - 1) // 2
    DIST = FEATS // 2 + 1
    NPC = 9
    CHUNKS = FEATS // NPC
    ROWS = [DIST * min(NPC, FEATS - 1 - NPC * c) for c in range(CHUNKS)]
    NUMC = NUM // P
    H0, H1, H2 = bot_w0.shape[1], bot_w1.shape[1], bot_w2.shape[1]
    G0, G1 = top_w0.shape[1], top_w1.shape[1]
    LEAK = 0.01

    BOT = (H0 + H1 + H2) // P
    TOP0, TOP1 = G0 // P, G1 // P
    TOP = 4

    def chunks_before(block):
        if block <= BOT:
            return block
        t, i = divmod(block - BOT, TOP)
        return BOT + (TOP0 + TOP1 + 1) * t + (0, 2, 4, 6)[i]

    DOT_GROUPS = {0: (0,), 1: (1,), 2: (2, 3), 3: (4,), 4: (5,), 5: (6, 7)}
    NUM_PAIRS, TOP0_PAIRS, TOP1_PAIR, TOP2_PAIR = (6, 7), (8, 9), 11, 12

    def row(n, m):
        return n * (FEATS - 1) - n * (n - 1) // 2 + m - n - 1

    PIECES = []
    for n in range(FEATS - 1):
        PIECES.append((row(n, n + 1), min(DIST, FEATS - 1 - n), n // NPC, n % NPC * DIST, 1))
    for k in range(FEATS - 1 - DIST):
        for c in range(CHUNKS):
            lo, hi = max(k + DIST, NPC * c), min(FEATS - 1, NPC * c + NPC)
            if lo < hi:
                PIECES.append((row(k, lo + 1), hi - lo, c, (lo - NPC * c) * DIST + FEATS + k - lo - 1, DIST - 1))

    COLUMNS, at = {}, 0
    for name, count in (("proj", NF), ("bot0", H0 // P), ("bot1", H1 // P), ("bot2", H2 // P),
                        ("top0", TOP0), ("top1", TOP1), ("last", TOP1)):
        COLUMNS[name] = slice(at, at + count)
        at += count
    NCOL = at

    table_rows = tables.rearrange("f v e -> (f v) e")

    with ExitStack() as ctx:
        def sb(name, shape, dt=fp32):
            return ctx.enter_context(nc.sbuf_tensor(name, shape, dt))

        def pb(name, shape):
            return ctx.enter_context(nc.psum_tensor(name, shape, fp32))

        def sem(name):
            return ctx.enter_context(nc.semaphore(name))

        cat = sb("cat", [P, TILES, NF], i32)
        first_row = sb("first_row", [P, NF], i32)
        wrap = sb("wrap", [P, TILES, NF])
        wrapped = sb("wrapped", [P, TILES, NF])
        clamped = sb("clamped", [P, TILES, NF])
        index = sb("index", [P, TILES, NF], i32)
        ident = sb("ident", [P, P])
        num = sb("num", [P, TILES, NUM])
        numT = sb("numT", [P, NUMC, BATCH])
        wp = sb("wp", [P, NF, P])
        wb0 = sb("wb0", [P, NUMC, H0])
        wb1 = sb("wb1", [P, H0 // P, H1])
        wb2 = sb("wb2", [P, H1 // P, H2])
        rows = sb("rows", [NCOL, P])
        cols = sb("cols", [P, NCOL])
        bt2 = sb("bt2", [1, 1])
        wt0 = sb("wt0", [P, CHUNKS, G0])
        wt0n = sb("wt0n", [P, NUMC, G0])
        wt1 = sb("wt1", [P, G0 // P, G1])
        hb0 = sb("hb0", [P, H0 // P, BATCH])
        hb1 = sb("hb1", [P, H1 // P, BATCH])
        xbot = sb("xbot", [P, BATCH])
        emb = sb("emb", [P, NF, EMB])
        embT = sb("embT", [P, 2, P])
        feats = [sb(f"feats{i}", [P, P, SLOTS]) for i in range(2)]
        dots = sb("dots", [SLOTS, FEATS, P])
        inter = [sb(f"inter{i}", [P, CHUNKS, P]) for i in range(2)]
        ht0 = sb("ht0", [P, G0 // P, P])
        ht1 = sb("ht1", [P, G1 // P, P])
        bot_pre = sb("bot_pre", [P, 2, BATCH])
        top0_pre = sb("top0_pre", [P, G0 // P, P])
        top1_pre = sb("top1_pre", [P, G1 // P, P])
        score = sb("score", [1, BATCH])

        ps_t = pb("ps_t", [P, 4, P])[:, 0, :]
        ps_p = [pb(f"ps_p{i}", [P, 4, P])[:, 0:2, :] for i in range(2)]
        ps_g = [pb(f"ps_g{i}", [P, GROUP, P]) for i in range(BANKS)]
        ps_h = [pb(f"ps_h{i}", [P, 512]) for i in range(2)]

        cat_loaded = sem("cat_loaded")
        first_ready = sem("first_ready")
        index_step = sem("index_step")
        index_ready = sem("index_ready")
        num_loaded = sem("num_loaded")
        bot0_loaded = sem("bot0_loaded")
        bot1_loaded = sem("bot1_loaded")
        bot2_loaded = sem("bot2_loaded")
        rows_loaded = sem("rows_loaded")
        proj_loaded = sem("proj_loaded")
        top0_loaded = sem("top0_loaded")
        top1_loaded = sem("top1_loaded")
        top2_loaded = sem("top2_loaded")
        ident_zeroed = sem("ident_zeroed")
        ident_ready = sem("ident_ready")
        wp_padded_low = sem("wp_padded_low")
        wp_padded_high = sem("wp_padded_high")
        wt0_zeroed = sem("wt0_zeroed")
        feats_padded = sem("feats_padded")
        cols_transposed = sem("cols_transposed")
        cols_placed = sem("cols_placed")
        gathered = [sem(f"gathered{j}") for j in range(PAIRS)]
        num_transposed = sem("num_transposed")
        num_placed = sem("num_placed")
        hidden_done = sem("hidden_done")
        hidden_read = sem("hidden_read")
        bot_placed = sem("bot_placed")
        emb_transposed = sem("emb_transposed")
        emb_placed = sem("emb_placed")
        projected = sem("projected")
        feats_placed = sem("feats_placed")
        x_placed = sem("x_placed")
        dots_done = sem("dots_done")
        dots_by_dve = sem("dots_by_dve")
        dots_by_act = sem("dots_by_act")
        dots_written = sem("dots_written")
        relaid = sem("relaid")
        top0_placed = sem("top0_placed")
        top1_placed = sem("top1_placed")
        stored = sem("stored")

        block = ctx.enter_context(nc.Block())

        def by_sample(t):
            return feats[t % 2][:].rearrange("p (q g) n -> p g q n", g=QUAD)

        def dots_block(t, group, g):
            src = ps_g[(GROUPS * t + group) % BANKS][SLOTS * g:SLOTS * g + SLOTS, :, FEATS * g:FEATS * g + FEATS]
            q0 = QUADS * g + GROUP * group
            return dots[:, :, q0:q0 + GROUP], src.rearrange("n q m -> n m q")

        by_feature = scratch[0:FEATS * FEATS * P].rearrange("(n m b) -> n m b", n=FEATS, b=P)
        by_distance = scratch.rearrange("(n d b) -> n d b", n=FEATS, b=P)

        @block.sync
        def _(sp):
            sp.dma_start(cat[:], r_cat.rearrange("(t p) f -> p t f", p=P)).then_inc(cat_loaded, 16)
            for name, vec in (("bot0", bot_b0), ("proj", proj_b), ("bot1", bot_b1), ("bot2", bot_b2),
                              ("top0", top_b0), ("top1", top_b1), ("last", top_w2)):
                if name == "last":
                    vec = vec.rearrange("(c p) o -> c (p o)", p=P)
                elif name != "proj":
                    vec = vec.rearrange("(c p) -> c p", p=P)
                sp.dma_start(rows[COLUMNS[name], :], vec).then_inc(rows_loaded, 16)
            even_odd = proj_w.rearrange("(j two) e p -> two e j p", two=2)
            wp_pairs = wp[:].rearrange("q (j two) p -> q j two p", two=2)
            for half in range(2):
                sp.dma_start(wp_pairs[EMB * half:EMB * half + EMB, :, half, :],
                             even_odd[half]).then_inc(proj_loaded, 16)
            sp.dma_start(wb1[:], bot_w1.rearrange("(c p) h -> p c h", p=P)).then_inc(bot1_loaded, 16)
            sp.dma_start(wb2[:], bot_w2.rearrange("(c p) h -> p c h", p=P)).then_inc(bot2_loaded, 16)
            sp.wait_ge(gathered[1], 32)
            sp.dma_start(bt2[:], top_b2.rearrange("(p c) -> p c", p=1)).then_inc(top2_loaded, 16)
            sp.dma_start(wt0n[:], top_w0[INTER:INTER + NUM, :].rearrange("(c p) h -> p c h", p=P)
                         ).then_inc(top0_loaded, 16)
            sp.wait_ge(wt0_zeroed, 1)
            for first, count, c, part, step in PIECES:
                sp.dma_start(wt0[part:part + step * (count - 1) + 1:step, c, :], top_w0[first:first + count, :]
                             ).then_inc(top0_loaded, 16)
            sp.dma_start(wt1[:], top_w1.rearrange("(c p) h -> p c h", p=P)).then_inc(top1_loaded, 16)
            for t in range(TILES):
                sp.wait_ge(dots_by_dve, 2 * GROUPS * (t + 1))
                sp.wait_ge(dots_by_act, 2 * GROUPS * (t + 1))
                if t > 0:
                    sp.wait_ge(relaid, 16 * CHUNKS * t)
                sp.dma_start(by_feature, dots[0:FEATS]).then_inc(dots_written, 16)
                sp.wait_ge(dots_written, 16 * (t + 1))
                if t >= 2:
                    sp.wait_ge(hidden_done, BOT + TOP * (t - 2) + 2)
                for c, rows_c in enumerate(ROWS):
                    sp.dma_start(inter[t % 2][0:rows_c, c, :],
                                 by_distance[NPC * c:NPC * c + rows_c // DIST, 1:DIST + 1, :]).then_inc(relaid, 16)
            sp.wait_ge(hidden_read, chunks_before(BOT + TOP * TILES))
            sp.dma_start(out.rearrange("(o b) -> o b", o=1), score[:]).then_inc(stored, 16)
            sp.wait_ge(stored, 16)

        @block.gpsimd
        def _(pool):
            nc.gpsimd.iota(first_row[:], [[VOCAB, NF]], base=0, channel_multiplier=0).then_inc(first_ready, 1)
            nc.gpsimd.memset(ident[:], 0.0).then_inc(ident_zeroed, 1)
            pool.wait_ge(ident_zeroed, 1)
            nc.gpsimd.affine_select(out=ident[:], in_=ident[:], compare_op=ALU.not_equal, fill=1.0, base=0,
                                    pattern=[[-1, P]], channel_multiplier=1).then_inc(ident_ready, 1)
            wp_pairs = wp[:].rearrange("q (j two) p -> q j two p", two=2)
            pool.wait_ge(ident_ready, 1)
            nc.gpsimd.memset(wp_pairs[EMB:P, :, 0, :], 0.0).then_inc(wp_padded_low, 1)
            pool.wait_ge(wp_padded_low, 1)
            pool.wait_ge(index_ready, 1)
            for t in range(TILES):
                for f in range(NF):
                    if t > 0 and f % 2 == 0:
                        pool.wait_ge(emb_transposed, PAIRS * (t - 1) + f // 2 + 1)
                    nc.gpsimd.indirect_dma_start(
                        emb[:, f, :], None, table_rows,
                        bass.IndirectOffsetOnAxis(ap=index[:, t, f:f + 1].bitcast(u32), axis=0),
                    ).then_inc(gathered[f // 2], 16)

        @block.scalar
        def _(act):
            act.dma_start(num[:], r_num.rearrange("(t p) c -> p t c", p=P)).then_inc(num_loaded, 16)
            act.dma_start(wb0[:], bot_w0.rearrange("(c p) h -> p c h", p=P)).then_inc(bot0_loaded, 16)

            def bias(name, h):
                return cols[:, COLUMNS[name].start + h:COLUMNS[name].start + h + 1]

            def add_bias(dst, src, column):
                return nc.scalar.activation(dst, src, ACT.Identity, bias=column)

            def bottom(i, name, h):
                act.wait_ge(hidden_done, i + 1)
                if i >= 2:
                    act.wait_ge(bot_placed, i - 1)
                add_bias(bot_pre[:, i % 2, :], ps_h[i % 2][:], bias(name, h)).then_inc(hidden_read, 1)

            def place_x(t):
                if t >= 2:
                    act.wait_ge(dots_done, GROUPS * (t - 1))
                nc.scalar.copy(by_sample(t)[:, :, :, 0],
                               xbot[:, P * t:P * t + P].rearrange("p (g q) -> p g q", g=QUAD)).then_inc(x_placed, 1)

            def place_emb(k):
                act.wait_ge(emb_transposed, k + 1)
                if k >= 2:
                    act.wait_ge(projected, k - 1)
                nc.scalar.copy(embT[:, k % 2, :], ps_t).then_inc(emb_placed, 1)

            def place_dots(t, group):
                act.wait_ge(dots_done, GROUPS * t + group + 1)
                if group == 0 and t > 0:
                    act.wait_ge(dots_written, 16 * t)
                for g in (2, 3):
                    dst, src = dots_block(t, group, g)
                    nc.scalar.copy(dst, src).then_inc(dots_by_act, 1)

            def top0(t, half):
                block = BOT + TOP * t + half
                act.wait_ge(hidden_done, block + 1)
                if t > 0 and half == 0:
                    act.wait_ge(top0_placed, TOP0 * t)
                for i in range(2):
                    h = 2 * half + i
                    add_bias(top0_pre[:, h, :], ps_h[block % 2][:, P * i:P * i + P], bias("top0", h)
                             ).then_inc(hidden_read, 1)

            def top1(t):
                block = BOT + TOP * t + 2
                act.wait_ge(hidden_done, block + 1)
                if t > 0:
                    act.wait_ge(top1_placed, TOP1 * t)
                for h in range(TOP1):
                    add_bias(top1_pre[:, h, :], ps_h[block % 2][:, P * h:P * h + P], bias("top1", h)
                             ).then_inc(hidden_read, 1)

            def top2(t):
                block = BOT + TOP * t + 3
                act.wait_ge(hidden_done, block + 1)
                if t == 0:
                    act.wait_ge(top2_loaded, 16)
                nc.scalar.activation(score[0:1, P * t:P * t + P], ps_h[block % 2][0:1, 0:P], ACT.Sigmoid,
                                     bias=bt2[:]).then_inc(hidden_read, 1)

            nc.scalar.preload_act_table_set("sigmoid_and_others")
            act.wait_ge(cols_placed, 1)
            for h in range(H0 // P):
                bottom(h, "bot0", h)
            for t in range(TILES):
                if t > 0:
                    place_x(t)
                for j in range(PAIRS):
                    place_emb(PAIRS * t + j)
                    if t == 0:
                        if j in (2, 4):
                            h = j // 2 - 1
                            bottom(H0 // P + h, "bot1", h)
                        if j == 5:
                            bottom(H0 // P + H1 // P, "bot2", 0)
                            act.wait_ge(bot_placed, BOT)
                            place_x(0)
                    else:
                        for group in DOT_GROUPS.get(j, ()):
                            place_dots(t - 1, group)
                    if t >= 2:
                        if j in TOP0_PAIRS:
                            top0(t - 2, TOP0_PAIRS.index(j))
                        if j == TOP1_PAIR:
                            top1(t - 2)
                        if j == TOP2_PAIR:
                            top2(t - 2)
            for group in range(GROUPS):
                place_dots(TILES - 1, group)
            for t in (TILES - 2, TILES - 1):
                for half in range(2):
                    top0(t, half)
                top1(t)
                top2(t)

        @block.vector
        def _(dve):
            dve.wait_ge(cat_loaded, 16)
            nc.vector.tensor_scalar(wrap[:], cat[:], 0.0, float(VOCAB), ALU.is_lt, ALU.mult).then_inc(index_step, 1)
            dve.wait_ge(index_step, 1)
            nc.vector.tensor_tensor(wrapped[:], wrap[:], cat[:], ALU.add).then_inc(index_step, 1)
            dve.wait_ge(index_step, 2)
            nc.vector.tensor_scalar(clamped[:], wrapped[:], float(VOCAB - 1), 0.0, ALU.min, ALU.max
                                    ).then_inc(index_step, 1)
            dve.wait_ge(index_step, 3)
            dve.wait_ge(first_ready, 1)
            nc.vector.tensor_tensor(index[:], clamped[:], first_row[:].unsqueeze(1).broadcast_to([P, TILES, NF]),
                                    ALU.add).then_inc(index_ready, 1)
            wp_pairs = wp[:].rearrange("q (j two) p -> q j two p", two=2)
            nc.vector.memset(wp_pairs[0:EMB, :, 1, :], 0.0).then_inc(wp_padded_high, 1)
            dve.wait_ge(cols_transposed, 1)
            nc.vector.tensor_copy(cols[:], ps_t[:, 0:NCOL]).then_inc(cols_placed, 1)
            for c in range(NUMC):
                dve.wait_ge(num_transposed, c + 1)
                nc.vector.tensor_copy(numT[:, c, :], ps_g[c][:].rearrange("p q b -> p (q b)")).then_inc(num_placed, 1)
            nc.vector.memset(wt0[:], 0.0).then_inc(wt0_zeroed, 1)

            def place_feats(k):
                t, j = k // PAIRS, k % PAIRS
                dve.wait_ge(projected, k + 1)
                if t >= 2 and j == 0:
                    dve.wait_ge(dots_done, GROUPS * (t - 1))
                nc.vector.tensor_tensor(
                    by_sample(t)[:, :, :, 2 * j + 1:2 * j + 3],
                    ps_p[k % 2].rearrange("p f (g q) -> p g q f", g=QUAD),
                    cols[:, 2 * j:2 * j + 2].unsqueeze(1).unsqueeze(1).broadcast_to([P, QUAD, QUADS, 2]),
                    ALU.add).then_inc(feats_placed, 1)

            def place_dots(t, group):
                dve.wait_ge(dots_done, GROUPS * t + group + 1)
                if group == 0 and t > 0:
                    dve.wait_ge(dots_written, 16 * t)
                for g in (0, 1):
                    dst, src = dots_block(t, group, g)
                    nc.vector.tensor_copy(dst, src).then_inc(dots_by_dve, 1)

            def leaky(dst, pre):
                return nc.vector.scalar_tensor_tensor(out=dst, in0=pre, scalar=LEAK, in1=pre,
                                                      op0=ALU.mult, op1=ALU.max)

            def bottom(i, dst):
                dve.wait_ge(hidden_read, i + 1)
                leaky(dst, bot_pre[:, i % 2, :]).then_inc(bot_placed, 1)

            def top0(t, half):
                if t > 0 and half == 0:
                    dve.wait_ge(hidden_done, BOT + TOP * (t - 1) + 3)
                for h in (2 * half, 2 * half + 1):
                    dve.wait_ge(hidden_read, chunks_before(BOT + TOP * t) + h + 1)
                    leaky(ht0[:, h, :], top0_pre[:, h, :]).then_inc(top0_placed, 1)

            def top1(t):
                if t > 0:
                    dve.wait_ge(hidden_done, BOT + TOP * t)
                for h in range(TOP1):
                    dve.wait_ge(hidden_read, chunks_before(BOT + TOP * t + 2) + h + 1)
                    leaky(ht1[:, h, :], top1_pre[:, h, :]).then_inc(top1_placed, 1)

            for h in range(H0 // P):
                bottom(h, hb0[:, h, :])
            for buf in feats:
                last = nc.vector.memset(buf[:, :, FEATS:SLOTS], 0.0)
            last.then_inc(feats_padded, 1)
            dve.wait_ge(cols_placed, 1)
            for t in range(TILES):
                for j in range(PAIRS):
                    k = PAIRS * t + j
                    if k > 0:
                        place_feats(k - 1)
                    if t == 0:
                        if j in (2, 4):
                            h = j // 2 - 1
                            bottom(H0 // P + h, hb1[:, h, :])
                        if j == 5:
                            bottom(H0 // P + H1 // P, xbot[:])
                    else:
                        for group in DOT_GROUPS.get(j, ()):
                            place_dots(t - 1, group)
                    if t >= 2:
                        if j in TOP0_PAIRS:
                            top0(t - 2, TOP0_PAIRS.index(j))
                        if j == TOP1_PAIR:
                            top1(t - 2)
            place_feats(PAIRS * TILES - 1)
            for group in range(GROUPS):
                place_dots(TILES - 1, group)
            for t in (TILES - 2, TILES - 1):
                for half in range(2):
                    top0(t, half)
                top1(t)

        @block.tensor
        def _(pe):
            def transpose_pair(k):
                t, j = k // PAIRS, k % PAIRS
                pe.wait_ge(gathered[j], 32 * (t + 1))
                if k > 0:
                    pe.wait_ge(emb_placed, k)
                nc.tensor.transpose(ps_t, emb[:, 2 * j:2 * j + 2, :].rearrange("p f e -> p (f e)"),
                                    ident[:]).then_inc(emb_transposed, 1)

            def project_pair(k):
                j = k % PAIRS
                pe.wait_ge(emb_placed, k + 1)
                if k >= 2:
                    pe.wait_ge(feats_placed, k - 1)
                for f in range(2):
                    last = nc.tensor.matmul(ps_p[k % 2][:, f, :], wp[:, 2 * j + f, :], embT[:, k % 2, :],
                                            start=True, stop=True)
                last.then_inc(projected, 1)

            def free_bank(block):
                if block >= 2:
                    pe.wait_ge(hidden_read, chunks_before(block - 1))

            def bottom(i, w, h, x, start, stop):
                chunks = w.shape[1]
                for c in range(start, stop):
                    last = nc.tensor.matmul(ps_h[i % 2][:], w[:, c, P * h:P * h + P], x[:, c, :],
                                            start=(c == 0), stop=(c == chunks - 1))
                if stop == chunks:
                    last.then_inc(hidden_done, 1)

            def dot_group(t, group):
                buf = feats[t % 2]
                bank = GROUPS * t + group
                if group == 0:
                    pe.wait_ge(feats_placed, PAIRS * (t + 1))
                    pe.wait_ge(x_placed, t + 1)
                if bank >= BANKS:
                    pe.wait_ge(dots_by_dve, 2 * (bank - BANKS + 1))
                    pe.wait_ge(dots_by_act, 2 * (bank - BANKS + 1))
                for q in range(GROUP):
                    pos = QUAD * (GROUP * group + q)
                    four = buf[:, pos:pos + QUAD, :]
                    last = nc.tensor.matmul(ps_g[bank % BANKS][:, q, 0:QUAD * FEATS],
                                            four.rearrange("p g n -> p (g n)"), four[:, :, 0:FEATS],
                                            start=True, stop=True)
                last.then_inc(dots_done, 1)

            def top0_num(t, half):
                block = BOT + TOP * t + half
                free_bank(block)
                for i in range(2):
                    cs = slice(P * (2 * half + i), P * (2 * half + i) + P)
                    for c in range(NUMC):
                        nc.tensor.matmul(ps_h[block % 2][:, P * i:P * i + P], wt0n[:, c, cs],
                                         numT[:, c, P * t:P * t + P], start=(i == 0 and c == 0), stop=False)

            def top0(t, half):
                block = BOT + TOP * t + half
                if half == 0:
                    pe.wait_ge(relaid, 16 * CHUNKS * (t + 1))
                for i in range(2):
                    cs = slice(P * (2 * half + i), P * (2 * half + i) + P)
                    for c in range(CHUNKS):
                        last = nc.tensor.matmul(ps_h[block % 2][:, P * i:P * i + P], wt0[0:ROWS[c], c, cs],
                                                inter[t % 2][0:ROWS[c], c, :],
                                                start=False, stop=(i == 1 and c == CHUNKS - 1))
                last.then_inc(hidden_done, 1)

            def top1(t):
                block = BOT + TOP * t + 2
                free_bank(block)
                for h in range(TOP1):
                    for c in range(TOP0):
                        if h == 0:
                            pe.wait_ge(top0_placed, TOP0 * t + c + 1)
                        last = nc.tensor.matmul(ps_h[block % 2][:, P * h:P * h + P], wt1[:, c, P * h:P * h + P],
                                                ht0[:, c, :], start=(h == 0 and c == 0),
                                                stop=(h == TOP1 - 1 and c == TOP0 - 1))
                last.then_inc(hidden_done, 1)

            def top2(t):
                block = BOT + TOP * t + 3
                free_bank(block)
                for c in range(TOP1):
                    pe.wait_ge(top1_placed, TOP1 * t + c + 1)
                    at = COLUMNS["last"].start + c
                    last = nc.tensor.matmul(ps_h[block % 2][0:1, 0:P], cols[:, at:at + 1], ht1[:, c, :],
                                            start=(c == 0), stop=(c == TOP1 - 1))
                last.then_inc(hidden_done, 1)

            pe.wait_ge(ident_ready, 1)
            pe.wait_ge(num_loaded, 16)
            for c in range(NUMC):
                for t in range(TILES):
                    last = nc.tensor.transpose(ps_g[c][:, t, :], num[:, t, P * c:P * c + P], ident[:])
                last.then_inc(num_transposed, 1)
            pe.wait_ge(rows_loaded, 16 * len(COLUMNS))
            nc.tensor.transpose(ps_t[:, 0:NCOL], rows[:], ident[0:NCOL, 0:NCOL]).then_inc(cols_transposed, 1)
            pe.wait_ge(num_placed, NUMC)
            pe.wait_ge(bot0_loaded, 16)
            for h in range(H0 // P):
                free_bank(h)
                bottom(h, wb0, h, numT, 0, NUMC)
            for t in range(TILES):
                for j in range(PAIRS):
                    k = PAIRS * t + j
                    if k == 0:
                        pe.wait_ge(cols_placed, 1)
                    transpose_pair(k)
                    if k == 1:
                        pe.wait_ge(proj_loaded, 32)
                        pe.wait_ge(wp_padded_low, 1)
                        pe.wait_ge(wp_padded_high, 1)
                    if k > 0:
                        project_pair(k - 1)
                    if t == 0:
                        if j == 1:
                            pe.wait_ge(bot1_loaded, 16)
                            pe.wait_ge(bot_placed, H0 // P)
                        if 1 <= j <= 4:
                            h, half = (j - 1) // 2, (j - 1) % 2
                            if half == 0:
                                free_bank(H0 // P + h)
                            bottom(H0 // P + h, wb1, h, hb0, 2 * half, 2 * half + 2)
                        if j == 5:
                            pe.wait_ge(bot2_loaded, 16)
                            pe.wait_ge(bot_placed, H0 // P + H1 // P)
                            free_bank(H0 // P + H1 // P)
                            bottom(H0 // P + H1 // P, wb2, 0, hb1, 0, H1 // P)
                            pe.wait_ge(feats_padded, 1)
                    else:
                        for group in DOT_GROUPS.get(j, ()):
                            dot_group(t - 1, group)
                    if t >= 2:
                        if t == 2 and j == NUM_PAIRS[0]:
                            pe.wait_ge(top0_loaded, 16 * (len(PIECES) + 1))
                            pe.wait_ge(top1_loaded, 16)
                        if j in NUM_PAIRS:
                            top0_num(t - 2, NUM_PAIRS.index(j))
                        if j in TOP0_PAIRS:
                            top0(t - 2, TOP0_PAIRS.index(j))
                        if j == TOP1_PAIR:
                            top1(t - 2)
                        if j == TOP2_PAIR:
                            top2(t - 2)
            project_pair(PAIRS * TILES - 1)
            for group in range(GROUPS):
                dot_group(TILES - 1, group)
            for t in (TILES - 2, TILES - 1):
                for half in range(2):
                    top0_num(t, half)
                for half in range(2):
                    top0(t, half)
                top1(t)
                top2(t)


_INS = ["r_num", "r_cat", "L0_rec_tables", "L0_rec_proj_w", "L0_rec_proj_b",
        "L0_rec_bot_w0", "L0_rec_bot_b0", "L0_rec_bot_w1", "L0_rec_bot_b1", "L0_rec_bot_w2", "L0_rec_bot_b2",
        "L0_rec_top_w0", "L0_rec_top_b0", "L0_rec_top_w1", "L0_rec_top_b1", "L0_rec_top_w2", "L0_rec_top_b2"]


def kernel(**inputs):
    import numpy as _np
    import concourse.bacc as _bacc
    from concourse import mybir as _mybir
    from concourse.bass_utils import run_bass_kernel_spmd as _run

    nc = _bacc.Bacc("TRN2", target_bir_lowering=False, num_devices=1)
    arrays, args = {}, []
    for name in _INS:
        a = _np.ascontiguousarray(inputs[name])
        arrays[f"in_{name}_dram"] = a
        args.append(nc.dram_tensor(f"in_{name}_dram", a.shape, _mybir.dt.from_np(a.dtype), kind="ExternalInput").ap())
    feats = arrays["in_L0_rec_tables_dram"].shape[0] + 1
    part = 128
    args.append(nc.dram_tensor("scratch_dram", (feats * (feats + 1) * part,), _mybir.dt.float32,
                               kind="Internal").ap())
    batch = arrays["in_r_num_dram"].shape[0]
    args.append(nc.dram_tensor("out_0_dram", (batch,), _mybir.dt.float32, kind="ExternalOutput").ap())
    recommender_kernel(nc, *args)
    r = _run(nc, [arrays], core_ids=[0])
    return r.results[0]["out_0_dram"]
```

```python
import concourse.bass as bass
from concourse import mybir
from contextlib import ExitStack


def recommender_kernel(
    nc: bass.Bass,
    r_num: bass.AP,
    r_cat: bass.AP,
    tables: bass.AP,
    proj_w: bass.AP,
    proj_b: bass.AP,
    bot_w0: bass.AP,
    bot_b0: bass.AP,
    bot_w1: bass.AP,
    bot_b1: bass.AP,
    bot_w2: bass.AP,
    bot_b2: bass.AP,
    top_w0: bass.AP,
    top_b0: bass.AP,
    top_w1: bass.AP,
    top_b1: bass.AP,
    top_w2: bass.AP,
    top_b2: bass.AP,
    out: bass.AP,
):
    fp32 = mybir.dt.float32
    i32 = mybir.dt.int32
    u32 = mybir.dt.uint32
    ALU = mybir.AluOpType
    ACT = mybir.ActivationFunctionType

    P = 128
    BATCH, NUM = r_num.shape
    NF, VOCAB, EMB = tables.shape
    TILES = BATCH // P
    PAIRS = NF // 2
    FEATS = NF + 1
    SLOTS = 32
    QUAD = P // SLOTS
    QUADS = P // QUAD
    GROUP = 4
    GROUPS = QUADS // GROUP
    BANKS = 3
    INTER = FEATS * (FEATS - 1) // 2
    CHUNKS = []
    n = 0
    while n < FEATS - 1:
        ms = FEATS - 1 - n
        ns = min(P // ms, FEATS - 1 - n)
        CHUNKS.append((n, ns, ms))
        n += ns
    NUMC = NUM // P
    H0, H1, H2 = bot_w0.shape[1], bot_w1.shape[1], bot_w2.shape[1]
    G0, G1 = top_w0.shape[1], top_w1.shape[1]
    LEAK = 0.01

    BOT = (H0 + H1 + H2) // P
    TOP0, TOP1 = G0 // P, G1 // P
    TOP = 4

    def chunks_before(block):
        if block <= BOT:
            return block
        t, i = divmod(block - BOT, TOP)
        return BOT + (TOP0 + TOP1) * t + (0, 2, 4, 5)[i]

    SPLIT = 5
    WHOLE = PAIRS - SPLIT
    STEPS = [(t, j, None) for t in range(TILES) for j in range(PAIRS if t < TILES - 1 else WHOLE)]
    STEPS += [(TILES - 1, j, h) for h in range(2) for j in range(WHOLE, PAIRS)]

    def steps_done(t, group):
        if t < TILES - 1:
            return PAIRS * (t + 1)
        return len(STEPS) - (SPLIT if group < GROUPS // 2 else 0)

    def whole_plan(t):
        u = t - 1
        plan = {1: (("dots", u, 0),), 2: (("dots", u, 1), ("dots", u, 2)), 3: (("dots", u, 3),),
                4: (("dots", u, 4), ("dots", u, 5)), 5: (("dots", u, 6), ("dots", u, 7)),
                6: (("numbers", u, 0),), 7: (("numbers", u, 1),), 8: (("top0", u, 0), ("top0", u, 1)),
                9: (("top0", u, 2),), 10: (("top0", u, 3),), 11: (("top1", u, 0), ("top1", u, 1)),
                12: (("logit", u, 0),)}
        if t == TILES - 2:
            plan[12] += (("dots", t, 0),)
        return plan

    def last_plan(t):
        u = t - 1
        return {0: (("dots", u, 1), ("dots", u, 2)), 1: (("dots", u, 3), ("dots", u, 4)),
                2: (("dots", u, 5), ("dots", u, 6)), 3: (("dots", u, 7),),
                4: (("numbers", u, 0), ("numbers", u, 1)),
                5: (("top0", u, 0),), 6: (("top0", u, 1), ("top0", u, 2)), 7: (("top0", u, 3),),
                9: (("top1", u, 0),), 14: (("dots", t, 0),), 15: (("dots", t, 1),), 16: (("dots", t, 2),)}

    PLANS = [{}] + [whole_plan(t) for t in range(1, TILES - 1)] + [last_plan(TILES - 1)]
    OWN = 3

    def projected_at(k):
        def last_of_tile(i):
            return i + 1 == len(STEPS) or STEPS[i + 1][0] != STEPS[i][0]

        steps = [k - 1] if k > 0 and not last_of_tile(k - 1) else []
        return steps + [k] if last_of_tile(k) else steps

    def behind(k):
        t = STEPS[k][0]
        return PLANS[t].get(k - PAIRS * t, ())

    def row(n, m):
        return n * (FEATS - 1) - n * (n - 1) // 2 + m - n - 1

    COLUMNS, at = {}, 0
    for name, count in (("proj", NF), ("bot0", H0 // P), ("bot1", H1 // P), ("bot2", H2 // P),
                        ("top0", TOP0), ("top1", TOP1), ("last", TOP1)):
        COLUMNS[name] = slice(at, at + count)
        at += count
    NCOL = at

    table_rows = tables.rearrange("f v e -> (f v) e")

    with ExitStack() as ctx:
        def sb(name, shape, dt=fp32):
            return ctx.enter_context(nc.sbuf_tensor(name, shape, dt))

        def pb(name, shape):
            return ctx.enter_context(nc.psum_tensor(name, shape, fp32))

        def sem(name):
            return ctx.enter_context(nc.semaphore(name))

        cat = sb("cat", [P, TILES, NF], i32)
        first_row = sb("first_row", [P, NF], i32)
        wrap = sb("wrap", [P, TILES, NF])
        wrapped = sb("wrapped", [P, TILES, NF])
        index = sb("index", [P, TILES, NF], i32)
        cat_split = sb("cat_split", [P, 2, 2 * SPLIT], i32)
        wrap_split = sb("wrap_split", [P, 2, 2 * SPLIT])
        wrapped_split = sb("wrapped_split", [P, 2, 2 * SPLIT])
        index_split = sb("index_split", [P, 2, SPLIT], i32)
        ident = sb("ident", [P, P])
        num = sb("num", [P, TILES, NUM])
        numT = sb("numT", [P, NUMC, BATCH])
        wp = sb("wp", [P, NF, P])
        wp_odd = sb("wp_odd", [EMB, SPLIT, P])
        wb0 = sb("wb0", [P, NUMC, H0])
        wb1 = sb("wb1", [P, H0 // P, H1])
        wb2 = sb("wb2", [P, H1 // P, H2])
        rows = sb("rows", [NCOL, P])
        cols = sb("cols", [P, NCOL])
        bt2 = sb("bt2", [1, 1])
        wt0 = sb("wt0", [P, len(CHUNKS), G0])
        wt0n = sb("wt0n", [P, NUMC, G0])
        wt1 = sb("wt1", [P, G0 // P, G1])
        hb0 = sb("hb0", [P, H0 // P, BATCH])
        hb1 = sb("hb1", [P, H1 // P, BATCH])
        xbot = sb("xbot", [P, BATCH])
        emb = sb("emb", [P, NF, EMB])
        emb_split = sb("emb_split", [P, 2 * SPLIT, EMB])
        embT = sb("embT", [P, 2, P])
        feats = [sb(f"feats{i}", [P, P, SLOTS]) for i in range(2)]
        dots = sb("dots", [SLOTS, FEATS, P])
        inter = sb("inter", [P, len(CHUNKS), P])
        ht0 = sb("ht0", [P, G0 // P, P])
        ht1 = sb("ht1", [P, G1 // P, P])
        bot_pre = sb("bot_pre", [P, 2, BATCH])
        top0_pre = sb("top0_pre", [P, G0 // P, P])
        top1_pre = sb("top1_pre", [P, G1 // P, P])
        score = sb("score", [1, BATCH])

        ps_t = pb("ps_t", [P, 4, P])[:, 0, :]
        ps_p = [pb(f"ps_p{i}", [P, 4, P])[:, 0:2, :] for i in range(2)]
        ps_g = [pb(f"ps_g{i}", [P, GROUP, P]) for i in range(BANKS)]
        ps_h = [pb(f"ps_h{i}", [P, 512]) for i in range(2)]

        cat_loaded = sem("cat_loaded")
        later_cat_loaded = sem("later_cat_loaded")
        first_ready = sem("first_ready")
        index_step = sem("index_step")
        index_ready = sem("index_ready")
        split_loaded = sem("split_loaded")
        split_ready = sem("split_ready")
        num_loaded = sem("num_loaded")
        bot0_loaded = sem("bot0_loaded")
        bot1_loaded = sem("bot1_loaded")
        bot2_loaded = sem("bot2_loaded")
        rows_loaded = sem("rows_loaded")
        proj_loaded = sem("proj_loaded")
        odd_loaded = sem("odd_loaded")
        top0_loaded = sem("top0_loaded")
        top1_loaded = sem("top1_loaded")
        top2_loaded = sem("top2_loaded")
        ident_zeroed = sem("ident_zeroed")
        ident_ready = sem("ident_ready")
        wp_padded_low = sem("wp_padded_low")
        wp_padded_high = sem("wp_padded_high")
        wt0_zeroed = sem("wt0_zeroed")
        feats_padded = sem("feats_padded")
        cols_transposed = sem("cols_transposed")
        cols_placed = sem("cols_placed")
        gathered = [sem(f"gathered{j}") for j in range(PAIRS)]
        gathered_split = [sem(f"gathered_split{u}") for u in range(2 * SPLIT)]
        num_transposed = sem("num_transposed")
        num_placed = sem("num_placed")
        hidden_done = sem("hidden_done")
        hidden_read = sem("hidden_read")
        bot_placed = sem("bot_placed")
        emb_transposed = sem("emb_transposed")
        emb_placed = sem("emb_placed")
        projected = sem("projected")
        feats_placed = sem("feats_placed")
        x_placed = sem("x_placed")
        dots_done = sem("dots_done")
        dots_by_dve = sem("dots_by_dve")
        dots_by_act = sem("dots_by_act")
        relaid = [sem(f"relaid{c}") for c in range(len(CHUNKS))]
        top0_placed = sem("top0_placed")
        top1_placed = sem("top1_placed")
        logit_done = sem("logit_done")
        score_placed = sem("score_placed")
        stored = sem("stored")

        block = ctx.enter_context(nc.Block())

        def by_sample(t):
            return feats[t % 2][:].rearrange("p (q g) n -> p g q n", g=QUAD)

        def dots_block(t, group, g):
            src = ps_g[(GROUPS * t + group) % BANKS][SLOTS * g:SLOTS * g + SLOTS, :, FEATS * g:FEATS * g + FEATS]
            q0 = QUADS * g + GROUP * group
            return dots[:, :, q0:q0 + GROUP], src.rearrange("n q m -> n m q")

        @block.sync
        def _(sp):
            sp.dma_start(cat[:, 0, :], r_cat[0:P, :]).then_inc(cat_loaded, 16)
            for name, vec in (("bot0", bot_b0), ("proj", proj_b), ("bot1", bot_b1), ("bot2", bot_b2),
                              ("top0", top_b0), ("top1", top_b1), ("last", top_w2)):
                if name == "last":
                    vec = vec.rearrange("(c p) o -> c (p o)", p=P)
                elif name != "proj":
                    vec = vec.rearrange("(c p) -> c p", p=P)
                sp.dma_start(rows[COLUMNS[name], :], vec).then_inc(rows_loaded, 16)
            sp.dma_start(cat[:, 1:TILES, :], r_cat[P:BATCH, :].rearrange("(t p) f -> p t f", p=P)
                         ).then_inc(later_cat_loaded, 16)
            even_odd = proj_w.rearrange("(j two) e p -> two e j p", two=2)
            wp_pairs = wp[:].rearrange("q (j two) p -> q j two p", two=2)
            for half in range(2):
                sp.dma_start(wp_pairs[EMB * half:EMB * half + EMB, :, half, :],
                             even_odd[half]).then_inc(proj_loaded, 16)
            sp.dma_start(wb1[:], bot_w1.rearrange("(c p) h -> p c h", p=P)).then_inc(bot1_loaded, 16)
            sp.dma_start(wb2[:], bot_w2.rearrange("(c p) h -> p c h", p=P)).then_inc(bot2_loaded, 16)
            sp.wait_ge(gathered[1], 32)
            sp.dma_start(bt2[:], top_b2.rearrange("(p c) -> p c", p=1)).then_inc(top2_loaded, 16)
            sp.dma_start(wt0n[:], top_w0[INTER:INTER + NUM, :].rearrange("(c p) h -> p c h", p=P)
                         ).then_inc(top0_loaded, 16)
            sp.wait_ge(wt0_zeroed, 1)
            for c, (first, ns, ms) in enumerate(CHUNKS):
                for n in range(first, first + ns):
                    part, count = ms * (n - first) + n - first, FEATS - 1 - n
                    sp.dma_start(wt0[part:part + count, c, :], top_w0[row(n, n + 1):row(n, n + 1) + count, :]
                                 ).then_inc(top0_loaded, 16)
            sp.dma_start(wt1[:], top_w1.rearrange("(c p) h -> p c h", p=P)).then_inc(top1_loaded, 16)
            sp.dma_start(wp_odd[:], even_odd[1][:, WHOLE:PAIRS, :]).then_inc(odd_loaded, 16)
            halves = r_cat[P * (TILES - 1):BATCH, 2 * WHOLE:NF].rearrange("(g h q) f -> h g q f", g=QUAD, h=2)
            for feature in range(2):
                for half in range(2):
                    sp.dma_start(cat_split[P // 2 * feature:P // 2 * feature + P // 2, half, :],
                                 halves[half]).then_inc(split_loaded, 16)
            for t in range(TILES):
                sp.wait_ge(dots_by_dve, 2 * GROUPS * (t + 1))
                sp.wait_ge(dots_by_act, 2 * GROUPS * (t + 1))
                if t > 0:
                    sp.wait_ge(hidden_done, BOT + TOP * (t - 1) + 2)
                for c, (n, ns, ms) in enumerate(CHUNKS):
                    sp.dma_start(inter[0:ns * ms, c, :], dots[n:n + ns, n + 1:FEATS, :]).then_inc(relaid[c], 16)
            sp.wait_ge(score_placed, TILES)
            sp.dma_start(out.rearrange("(o b) -> o b", o=1), score[:]).then_inc(stored, 16)
            sp.wait_ge(stored, 16)

        @block.gpsimd
        def _(pool):
            nc.gpsimd.iota(first_row[:], [[VOCAB, NF]], base=0, channel_multiplier=0).then_inc(first_ready, 1)
            nc.gpsimd.memset(ident[:], 0.0).then_inc(ident_zeroed, 1)
            pool.wait_ge(ident_zeroed, 1)
            nc.gpsimd.affine_select(out=ident[:], in_=ident[:], compare_op=ALU.not_equal, fill=1.0, base=0,
                                    pattern=[[-1, P]], channel_multiplier=1).then_inc(ident_ready, 1)
            wp_pairs = wp[:].rearrange("q (j two) p -> q j two p", two=2)
            pool.wait_ge(ident_ready, 1)
            nc.gpsimd.memset(wp_pairs[EMB:P, :, 0, :], 0.0).then_inc(wp_padded_low, 1)
            pool.wait_ge(wp_padded_low, 1)
            for t, j, half in STEPS:
                if half is None:
                    if j == 0 and t < 2:
                        pool.wait_ge(index_ready, t + 1)
                    if t > 0:
                        pool.wait_ge(emb_transposed, PAIRS * (t - 1) + j + 1)
                    for f in (2 * j, 2 * j + 1):
                        nc.gpsimd.indirect_dma_start(
                            emb[:, f, :], None, table_rows,
                            bass.IndirectOffsetOnAxis(ap=index[:, t, f:f + 1].bitcast(u32), axis=0),
                        ).then_inc(gathered[j], 16)
                else:
                    i = j - WHOLE
                    u = SPLIT * half + i
                    if u == 0:
                        pool.wait_ge(split_ready, 2)
                    nc.gpsimd.indirect_dma_start(
                        emb_split[:, u, :], None, table_rows,
                        bass.IndirectOffsetOnAxis(ap=index_split[:, half, i:i + 1].bitcast(u32), axis=0),
                    ).then_inc(gathered_split[u], 16)

        @block.scalar
        def _(act):
            act.dma_start(num[:], r_num.rearrange("(t p) c -> p t c", p=P)).then_inc(num_loaded, 16)
            act.dma_start(wb0[:], bot_w0.rearrange("(c p) h -> p c h", p=P)).then_inc(bot0_loaded, 16)

            def bias(name, h):
                return cols[:, COLUMNS[name].start + h:COLUMNS[name].start + h + 1]

            def add_bias(dst, src, column):
                return nc.scalar.activation(dst, src, ACT.Identity, bias=column)

            def bottom(i, name, h):
                act.wait_ge(hidden_done, i + 1)
                if i >= 2:
                    act.wait_ge(bot_placed, i - 1)
                add_bias(bot_pre[:, i % 2, :], ps_h[i % 2][:], bias(name, h)).then_inc(hidden_read, 1)

            def place_x(t):
                if t >= 2:
                    act.wait_ge(dots_done, GROUPS * (t - 1))
                nc.scalar.copy(by_sample(t)[:, :, :, 0],
                               xbot[:, P * t:P * t + P].rearrange("p (g q) -> p g q", g=QUAD)).then_inc(x_placed, 1)

            def place_emb(k):
                act.wait_ge(emb_transposed, k + 1)
                if k >= 2:
                    act.wait_ge(projected, k - 1)
                rows_k = P if STEPS[k][2] is None else EMB
                nc.scalar.copy(embT[0:rows_k, k % 2, :], ps_t[0:rows_k, :]).then_inc(emb_placed, 1)

            def place_dots(t, group):
                act.wait_ge(dots_done, GROUPS * t + group + 1)
                if group == 0 and t > 0:
                    for c in range(len(CHUNKS)):
                        act.wait_ge(relaid[c], 16 * t)
                for g in (2, 3):
                    dst, src = dots_block(t, group, g)
                    nc.scalar.copy(dst, src).then_inc(dots_by_act, 1)

            def top0(t, half):
                block = BOT + TOP * t + half
                act.wait_ge(hidden_done, block + 1)
                if t > 0 and half == 0:
                    act.wait_ge(top0_placed, TOP0 * t)
                for i in range(2):
                    h = 2 * half + i
                    add_bias(top0_pre[:, h, :], ps_h[block % 2][:, P * i:P * i + P], bias("top0", h)
                             ).then_inc(hidden_read, 1)

            def top1(t, h):
                block = BOT + TOP * t + 2 + h
                act.wait_ge(hidden_done, block + 1)
                if t > 0 and h == 0:
                    act.wait_ge(top1_placed, TOP1 * t)
                add_bias(top1_pre[:, h, :], ps_h[block % 2][:, 0:P], bias("top1", h)).then_inc(hidden_read, 1)

            def logit(t):
                act.wait_ge(logit_done, t + 1)
                if t == 0:
                    act.wait_ge(top2_loaded, 16)
                nc.scalar.activation(score[0:1, P * t:P * t + P], ps_t[0:1, :], ACT.Sigmoid,
                                     bias=bt2[:]).then_inc(score_placed, 1)

            nc.scalar.preload_act_table_set("sigmoid_and_others")
            act.wait_ge(cols_placed, 1)
            for h in range(H0 // P):
                bottom(h, "bot0", h)
            for k, (t, j, half) in enumerate(STEPS):
                if t > 0 and k == PAIRS * t:
                    place_x(t)
                place_emb(k)
                if k in (2, 4):
                    h = k // 2 - 1
                    bottom(H0 // P + h, "bot1", h)
                if k == 5:
                    bottom(H0 // P + H1 // P, "bot2", 0)
                    act.wait_ge(bot_placed, BOT)
                    place_x(0)
                for what, u, i in behind(k):
                    if what == "logit":
                        logit(u)
                    if what == "dots":
                        place_dots(u, i)
                    if what == "top0" and i == len(CHUNKS) - 1:
                        top0(u, 0)
                        top0(u, 1)
                    if what == "top1":
                        top1(u, i)
            for group in range(OWN, GROUPS):
                place_dots(TILES - 1, group)
            top1(TILES - 2, 1)
            for half in range(2):
                top0(TILES - 1, half)
            logit(TILES - 2)
            for h in range(TOP1):
                top1(TILES - 1, h)
            logit(TILES - 1)

        @block.vector
        def _(dve):
            def wrap_index(part, into, wraps, cats):
                nc.vector.tensor_scalar(wraps, cats, 0.0, float(VOCAB), ALU.is_lt, ALU.mult).then_inc(index_step, 1)
                dve.wait_ge(index_step, 2 * part + 1)
                nc.vector.scalar_tensor_tensor(out=into, in0=cats, scalar=-float(VOCAB), in1=wraps,
                                               op0=ALU.max, op1=ALU.add).then_inc(index_step, 1)
                dve.wait_ge(index_step, 2 * part + 2)

            def finish_index(into, within, first):
                return nc.vector.scalar_tensor_tensor(out=into, in0=within, scalar=float(VOCAB - 1), in1=first,
                                                      op0=ALU.min, op1=ALU.add)

            dve.wait_ge(cat_loaded, 16)
            wrap_index(0, wrapped[:, 0, :], wrap[:, 0, :], cat[:, 0, :])
            dve.wait_ge(first_ready, 1)
            finish_index(index[:, 0, :], wrapped[:, 0, :], first_row[:]).then_inc(index_ready, 1)
            wp_pairs = wp[:].rearrange("q (j two) p -> q j two p", two=2)
            nc.vector.memset(wp_pairs[0:EMB, :, 1, :], 0.0).then_inc(wp_padded_high, 1)
            dve.wait_ge(cols_transposed, 1)
            nc.vector.tensor_copy(cols[:], ps_t[:, 0:NCOL]).then_inc(cols_placed, 1)
            for c in range(NUMC):
                dve.wait_ge(num_transposed, c + 1)
                nc.vector.tensor_copy(numT[:, c, :], ps_g[c][:].rearrange("p q b -> p (q b)")).then_inc(num_placed, 1)
            nc.vector.memset(wt0[:], 0.0).then_inc(wt0_zeroed, 1)
            dve.wait_ge(later_cat_loaded, 16)
            wrap_index(1, wrapped[:, 1:TILES, :], wrap[:, 1:TILES, :], cat[:, 1:TILES, :])
            finish_index(index[:, 1:TILES, :], wrapped[:, 1:TILES, :],
                         first_row[:].unsqueeze(1).broadcast_to([P, TILES - 1, NF])).then_inc(index_ready, 1)

            def split_indices():
                dve.wait_ge(split_loaded, 64)
                wrap_index(2, wrapped_split[:], wrap_split[:], cat_split[:])
                for f in range(2):
                    part = slice(P // 2 * f, P // 2 * f + P // 2)
                    finish_index(index_split[part], wrapped_split[part, :, f:2 * SPLIT:2],
                                 first_row[part, 2 * WHOLE + f:NF:2].unsqueeze(1).broadcast_to([P // 2, 2, SPLIT])
                                 ).then_inc(split_ready, 1)

            def place_feats(k):
                t, j, half = STEPS[k]
                dve.wait_ge(projected, k + 1)
                if t >= 2 and k == PAIRS * t:
                    dve.wait_ge(dots_done, GROUPS * (t - 1))
                qs = slice(0, QUADS) if half is None else slice(QUADS // 2 * half, QUADS // 2 * (half + 1))
                count = qs.stop - qs.start
                nc.vector.tensor_tensor(
                    by_sample(t)[:, :, qs, 2 * j + 1:2 * j + 3],
                    ps_p[k % 2][:, :, 0:QUAD * count].rearrange("p f (g q) -> p g q f", g=QUAD),
                    cols[:, 2 * j:2 * j + 2].unsqueeze(1).unsqueeze(1).broadcast_to([P, QUAD, count, 2]),
                    ALU.add).then_inc(feats_placed, 1)

            def place_dots(t, group):
                dve.wait_ge(dots_done, GROUPS * t + group + 1)
                if group == 0 and t > 0:
                    for c in range(len(CHUNKS)):
                        dve.wait_ge(relaid[c], 16 * t)
                for g in (0, 1):
                    dst, src = dots_block(t, group, g)
                    nc.vector.tensor_copy(dst, src).then_inc(dots_by_dve, 1)

            def leaky(dst, pre):
                return nc.vector.scalar_tensor_tensor(out=dst, in0=pre, scalar=LEAK, in1=pre,
                                                      op0=ALU.mult, op1=ALU.max)

            def bottom(i, dst):
                dve.wait_ge(hidden_read, i + 1)
                leaky(dst, bot_pre[:, i % 2, :]).then_inc(bot_placed, 1)

            def top0(t, half):
                if t > 0 and half == 0:
                    dve.wait_ge(hidden_done, BOT + TOP * (t - 1) + 4)
                for h in (2 * half, 2 * half + 1):
                    dve.wait_ge(hidden_read, chunks_before(BOT + TOP * t) + h + 1)
                    leaky(ht0[:, h, :], top0_pre[:, h, :]).then_inc(top0_placed, 1)

            def top1(t, h):
                if t > 0 and h == 0:
                    dve.wait_ge(logit_done, t)
                dve.wait_ge(hidden_read, chunks_before(BOT + TOP * t + 2 + h) + 1)
                leaky(ht1[:, h, :], top1_pre[:, h, :]).then_inc(top1_placed, 1)

            for h in range(H0 // P):
                bottom(h, hb0[:, h, :])
            for buf in feats:
                last = nc.vector.memset(buf[:, :, FEATS:SLOTS], 0.0)
            last.then_inc(feats_padded, 1)
            dve.wait_ge(cols_placed, 1)
            for k, (t, j, half) in enumerate(STEPS):
                for i in projected_at(k):
                    place_feats(i)
                if k in (2, 4):
                    h = k // 2 - 1
                    bottom(H0 // P + h, hb1[:, h, :])
                if k == 5:
                    bottom(H0 // P + H1 // P, xbot[:])
                if k == WHOLE:
                    split_indices()
                for what, u, i in behind(k):
                    if what == "dots":
                        place_dots(u, i)
                    if what == "top0" and i == len(CHUNKS) - 1:
                        top0(u, 0)
                        top0(u, 1)
                    if what == "top1":
                        top1(u, i)
            for group in range(OWN, GROUPS):
                place_dots(TILES - 1, group)
            top1(TILES - 2, 1)
            for half in range(2):
                top0(TILES - 1, half)
            for h in range(TOP1):
                top1(TILES - 1, h)

        @block.tensor
        def _(pe):
            def transpose_pair(k):
                t, j, half = STEPS[k]
                if half is None:
                    pe.wait_ge(gathered[j], 32 * (t + 1))
                    rows_k, src = P, emb[:, 2 * j:2 * j + 2, :].rearrange("p f e -> p (f e)")
                else:
                    u = SPLIT * half + j - WHOLE
                    pe.wait_ge(gathered_split[u], 16)
                    rows_k, src = EMB, emb_split[:, u, :]
                if k > 0:
                    pe.wait_ge(emb_placed, k)
                    for what, u, _ in behind(k - 1):
                        if what == "logit":
                            pe.wait_ge(score_placed, u + 1)
                nc.tensor.transpose(ps_t[0:rows_k, :], src, ident[:]).then_inc(emb_transposed, 1)

            def project_pair(k):
                t, j, half = STEPS[k]
                pe.wait_ge(emb_placed, k + 1)
                if k >= 2:
                    pe.wait_ge(feats_placed, k - 1)
                if half == 0 and j == WHOLE:
                    pe.wait_ge(odd_loaded, 16)
                for f in range(2):
                    if half is None:
                        last = nc.tensor.matmul(ps_p[k % 2][:, f, :], wp[:, 2 * j + f, :], embT[:, k % 2, :],
                                                start=True, stop=True)
                    else:
                        weights = wp[0:EMB, 2 * j, :] if f == 0 else wp_odd[:, j - WHOLE, :]
                        last = nc.tensor.matmul(ps_p[k % 2][:, f, 0:P // 2], weights,
                                                embT[0:EMB, k % 2, P // 2 * f:P // 2 * f + P // 2],
                                                start=True, stop=True)
                last.then_inc(projected, 1)

            def free_bank(block):
                if block >= 2:
                    pe.wait_ge(hidden_read, chunks_before(block - 1))

            def bottom(i, w, h, x, start, stop):
                chunks = w.shape[1]
                for c in range(start, stop):
                    last = nc.tensor.matmul(ps_h[i % 2][:], w[:, c, P * h:P * h + P], x[:, c, :],
                                            start=(c == 0), stop=(c == chunks - 1))
                if stop == chunks:
                    last.then_inc(hidden_done, 1)

            def dot_group(t, group):
                buf = feats[t % 2]
                bank = GROUPS * t + group
                if group in (0, GROUPS // 2):
                    pe.wait_ge(feats_placed, steps_done(t, group))
                    pe.wait_ge(x_placed, t + 1)
                if bank >= BANKS:
                    pe.wait_ge(dots_by_dve, 2 * (bank - BANKS + 1))
                    pe.wait_ge(dots_by_act, 2 * (bank - BANKS + 1))
                for q in range(GROUP):
                    pos = QUAD * (GROUP * group + q)
                    four = buf[:, pos:pos + QUAD, :]
                    last = nc.tensor.matmul(ps_g[bank % BANKS][:, q, 0:QUAD * FEATS],
                                            four.rearrange("p g n -> p (g n)"), four[:, :, 0:FEATS],
                                            start=True, stop=True)
                last.then_inc(dots_done, 1)

            def top0_num(t, half):
                block = BOT + TOP * t + half
                free_bank(block)
                for i in range(2):
                    cs = slice(P * (2 * half + i), P * (2 * half + i) + P)
                    for c in range(NUMC):
                        nc.tensor.matmul(ps_h[block % 2][:, P * i:P * i + P], wt0n[:, c, cs],
                                         numT[:, c, P * t:P * t + P], start=(i == 0 and c == 0), stop=False)

            def top0(t, chunk):
                _, ns, ms = CHUNKS[chunk]
                pe.wait_ge(relaid[chunk], 16 * (t + 1))
                for h in range(TOP0):
                    block = BOT + TOP * t + h // 2
                    done = h % 2 == 1 and chunk == len(CHUNKS) - 1
                    last = nc.tensor.matmul(ps_h[block % 2][:, P * (h % 2):P * (h % 2) + P],
                                            wt0[0:ns * ms, chunk, P * h:P * h + P],
                                            inter[0:ns * ms, chunk, :], start=False, stop=done)
                    if done:
                        last.then_inc(hidden_done, 1)

            def top1(t, h):
                block = BOT + TOP * t + 2 + h
                free_bank(block)
                for c in range(TOP0):
                    if h == 0:
                        pe.wait_ge(top0_placed, TOP0 * t + c + 1)
                    last = nc.tensor.matmul(ps_h[block % 2][:, 0:P], wt1[:, c, P * h:P * h + P], ht0[:, c, :],
                                            start=(c == 0), stop=(c == TOP0 - 1))
                last.then_inc(hidden_done, 1)

            def logit(t, k):
                pe.wait_ge(emb_placed, k + 1)
                if t == TILES - 1:
                    pe.wait_ge(score_placed, t)
                for c in range(TOP1):
                    pe.wait_ge(top1_placed, TOP1 * t + c + 1)
                    at = COLUMNS["last"].start + c
                    last = nc.tensor.matmul(ps_t[0:1, :], cols[:, at:at + 1], ht1[:, c, :],
                                            start=(c == 0), stop=(c == TOP1 - 1))
                last.then_inc(logit_done, 1)

            pe.wait_ge(ident_ready, 1)
            pe.wait_ge(num_loaded, 16)
            for c in range(NUMC):
                for t in range(TILES):
                    last = nc.tensor.transpose(ps_g[c][:, t, :], num[:, t, P * c:P * c + P], ident[:])
                last.then_inc(num_transposed, 1)
            pe.wait_ge(rows_loaded, 16 * len(COLUMNS))
            nc.tensor.transpose(ps_t[:, 0:NCOL], rows[:], ident[0:NCOL, 0:NCOL]).then_inc(cols_transposed, 1)
            pe.wait_ge(num_placed, NUMC)
            pe.wait_ge(bot0_loaded, 16)
            for h in range(H0 // P):
                free_bank(h)
                bottom(h, wb0, h, numT, 0, NUMC)
            pe.wait_ge(cols_placed, 1)
            for k, (t, j, half) in enumerate(STEPS):
                transpose_pair(k)
                if k == 1:
                    pe.wait_ge(proj_loaded, 32)
                    pe.wait_ge(wp_padded_low, 1)
                    pe.wait_ge(wp_padded_high, 1)
                for i in projected_at(k):
                    project_pair(i)
                if k == 1:
                    pe.wait_ge(bot1_loaded, 16)
                    pe.wait_ge(bot_placed, H0 // P)
                if 1 <= k <= 4:
                    h, part = (k - 1) // 2, (k - 1) % 2
                    if part == 0:
                        free_bank(H0 // P + h)
                    bottom(H0 // P + h, wb1, h, hb0, 2 * part, 2 * part + 2)
                if k == 5:
                    pe.wait_ge(bot2_loaded, 16)
                    pe.wait_ge(bot_placed, H0 // P + H1 // P)
                    free_bank(H0 // P + H1 // P)
                    bottom(H0 // P + H1 // P, wb2, 0, hb1, 0, H1 // P)
                    pe.wait_ge(feats_padded, 1)
                for what, u, i in behind(k):
                    if what == "logit":
                        logit(u, k)
                    if what == "dots":
                        dot_group(u, i)
                    if what == "numbers":
                        if u == 0 and i == 0:
                            pe.wait_ge(top0_loaded, 16 * FEATS)
                            pe.wait_ge(top1_loaded, 16)
                        top0_num(u, i)
                    if what == "top0":
                        top0(u, i)
                    if what == "top1":
                        top1(u, i)
            for group in range(OWN, GROUPS):
                dot_group(TILES - 1, group)
            top1(TILES - 2, 1)
            for half in range(2):
                top0_num(TILES - 1, half)
            for chunk in range(len(CHUNKS)):
                top0(TILES - 1, chunk)
            logit(TILES - 2, len(STEPS) - 1)
            for h in range(TOP1):
                top1(TILES - 1, h)
            logit(TILES - 1, len(STEPS) - 1)


_INS = ["r_num", "r_cat", "L0_rec_tables", "L0_rec_proj_w", "L0_rec_proj_b",
        "L0_rec_bot_w0", "L0_rec_bot_b0", "L0_rec_bot_w1", "L0_rec_bot_b1", "L0_rec_bot_w2", "L0_rec_bot_b2",
        "L0_rec_top_w0", "L0_rec_top_b0", "L0_rec_top_w1", "L0_rec_top_b1", "L0_rec_top_w2", "L0_rec_top_b2"]


def kernel(**inputs):
    import numpy as _np
    import concourse.bacc as _bacc
    from concourse import mybir as _mybir
    from concourse.bass_utils import run_bass_kernel_spmd as _run

    nc = _bacc.Bacc("TRN2", target_bir_lowering=False, num_devices=1)
    arrays, args = {}, []
    for name in _INS:
        a = _np.ascontiguousarray(inputs[name])
        arrays[f"in_{name}_dram"] = a
        args.append(nc.dram_tensor(f"in_{name}_dram", a.shape, _mybir.dt.from_np(a.dtype), kind="ExternalInput").ap())
    batch = arrays["in_r_num_dram"].shape[0]
    args.append(nc.dram_tensor("out_0_dram", (batch,), _mybir.dt.float32, kind="ExternalOutput").ap())
    recommender_kernel(nc, *args)
    r = _run(nc, [arrays], core_ids=[0])
    return r.results[0]["out_0_dram"]
```
